# Optimizing a Trainium2 kernel written in Bass

```python
import numpy as np
import jax
import jax.numpy as jnp

def _softmax(x, axis=-1):
    return jax.nn.softmax(x, axis=axis)
def _gelu(x):
    return jax.nn.gelu(x, approximate=True)
def _silu(x):
    return jax.nn.silu(x)
def _sigmoid(x):
    return jax.nn.sigmoid(x)
def _layernorm(x, axis=-1, eps=1e-5):
    m = jnp.mean(x, axis=axis, keepdims=True)
    v = jnp.var(x, axis=axis, keepdims=True)
    return (x - m) / jnp.sqrt(v + eps)
def _scatter_add(tgt, idx, src, axis=0):
    return tgt.at[idx].add(src)
def _segment_sum(src, seg, n):
    return jax.ops.segment_sum(src, seg, n)

kernel_name = 'mk_conv_preact_d4_conv_nhwc768_17d6ec'

def setup_inputs(seed: int = 0):
    np.random.seed(seed)
    _w = jnp.asarray
    def _rec_inputs():
        import jax
        import jax.numpy as jnp
        _gk = jax.random.key(seed)
        x = -0.001003 + 1 * jax.random.normal(jax.random.fold_in(_gk, 1), (2, 32, 32, 768), jnp.float32)
        return x
    x = _rec_inputs()
    def _L0_conv_setup():
        import jax, jax.numpy as jnp
        import numpy as np
        D_HEAD = 64
        KV_GROUPS = 3
        KSIZE = 7

        def _win_idx(L, ksize):
            start = jnp.clip(jnp.arange(L) - ksize // 2, 0, L - ksize)
            return start[:, None] + jnp.arange(ksize)[None, :]

        def _natten2d(q, k, v, ksize):
            H, W = (q.shape[2], q.shape[3])
            ih = _win_idx(H, ksize)
            iw = _win_idx(W, ksize)
            kg = k[:, :, ih[:, None, :, None], iw[None, :, None, :], :]
            vg = v[:, :, ih[:, None, :, None], iw[None, :, None, :], :]
            logits = jnp.einsum('nhije,nhijabe->nhijab', q, kg)
            n_, nh = logits.shape[:2]
            a = jax.nn.softmax(logits.reshape(n_, nh, H, W, ksize * ksize), axis=-1)
            a = a.reshape(logits.shape)
            return jnp.einsum('nhijab,nhijabe->nhije', a, vg)

        def _to_heads(p, nh, e):
            n, h, w, _ = p.shape
            return p.reshape(n, h, w, nh, e).transpose(0, 3, 1, 2, 4)
        key = jax.random.key(seed)
        k1, k2, k3 = jax.random.split(key, 3)
        x = jax.random.normal(k1, (2, 32, 32, 768), dtype=jnp.float32)
        w_qkv = jax.random.normal(k2, (1280, 768), dtype=jnp.float32) * 0.02
        w_out = jax.random.normal(k3, (768, 768), dtype=jnp.float32) * 0.02
        return {'x': x, 'w_qkv': w_qkv, 'w_out': w_out}
    _L0_conv_all = _L0_conv_setup()
    _L0_conv_in = {k: v for k, v in _L0_conv_all.items() if k in ('w_qkv', 'w_out', )}
    del _L0_conv_all

    def _L1_conv_setup():
        import jax, jax.numpy as jnp
        import numpy as np
        NUM_HEADS = 12
        H = W = 64
        DIM = 768
        HEAD_DIM = DIM // NUM_HEADS

        def _get_rel_pos(size: int, rel_pos: jnp.ndarray) -> jnp.ndarray:
            coords = jnp.arange(size)[:, None] - jnp.arange(size)[None, :] + (size - 1)
            return rel_pos[coords]
        key = jax.random.key(seed)
        ks = jax.random.split(key, 7)
        return {'x': jax.random.normal(ks[0], (1, H, W, DIM), dtype=jnp.float32), 'qkv_w': jax.random.normal(ks[1], (3 * DIM, DIM), dtype=jnp.float32) * 0.02, 'qkv_b': jax.random.normal(ks[2], (3 * DIM,), dtype=jnp.float32) * 0.02, 'proj_w': jax.random.normal(ks[3], (DIM, DIM), dtype=jnp.float32) * 0.02, 'proj_b': jax.random.normal(ks[4], (DIM,), dtype=jnp.float32) * 0.02, 'rel_pos_h': jax.random.normal(ks[5], (2 * H - 1, HEAD_DIM), dtype=jnp.float32) * 0.02, 'rel_pos_w': jax.random.normal(ks[6], (2 * W - 1, HEAD_DIM), dtype=jnp.float32) * 0.02}
    _L1_conv_all = _L1_conv_setup()
    _L1_conv_in = {k: v for k, v in _L1_conv_all.items() if k in ('qkv_w', 'qkv_b', 'proj_w', 'proj_b', 'rel_pos_h', 'rel_pos_w', )}
    del _L1_conv_all

    def _L2_conv_setup():
        import jax, jax.numpy as jnp
        import numpy as np
        NUM_HEADS = 12
        key = jax.random.key(seed)
        k1, k2, k3 = jax.random.split(key, 3)
        dim = 768
        x = jax.random.normal(k1, (1, 64, 64, dim), dtype=jnp.float32)
        qkv_w = jax.random.normal(k2, (3 * dim, dim), dtype=jnp.float32) * dim ** (-0.5)
        qkv_b = jnp.zeros((3 * dim,), dtype=jnp.float32)
        proj_w = jax.random.normal(k3, (dim, dim), dtype=jnp.float32) * dim ** (-0.5)
        proj_b = jnp.zeros((dim,), dtype=jnp.float32)
        return {'x': x, 'qkv_w': qkv_w, 'qkv_b': qkv_b, 'proj_w': proj_w, 'proj_b': proj_b}
    _L2_conv_all = _L2_conv_setup()
    _L2_conv_in = {k: v for k, v in _L2_conv_all.items() if k in ('qkv_w', 'qkv_b', 'proj_w', 'proj_b', )}
    del _L2_conv_all

    def _L3_conv_setup():
        import jax, jax.numpy as jnp
        import numpy as np

        def _rel_pos_table(size, rel_pos):
            coords = jnp.arange(size)[:, None] - jnp.arange(size)[None, :] + (size - 1)
            return rel_pos[coords]
        key = jax.random.key(seed)
        ks = jax.random.split(key, 7)
        N, H, W, C = (8, 32, 32, 768)
        hd = C // 12
        return {'x': jax.random.normal(ks[0], (N, H, W, C), jnp.float32), 'w_qkv': jax.random.normal(ks[1], (C, 3 * C), jnp.float32) * 0.02, 'b_qkv': jax.random.normal(ks[2], (3 * C,), jnp.float32) * 0.02, 'w_proj': jax.random.normal(ks[3], (C, C), jnp.float32) * 0.02, 'b_proj': jax.random.normal(ks[4], (C,), jnp.float32) * 0.02, 'rel_pos_h': jax.random.normal(ks[5], (2 * H - 1, hd), jnp.float32) * 0.02, 'rel_pos_w': jax.random.normal(ks[6], (2 * W - 1, hd), jnp.float32) * 0.02, 'nb_heads': 12}
    _L3_conv_all = _L3_conv_setup()
    _L3_conv_in = {k: v for k, v in _L3_conv_all.items() if k in ('w_qkv', 'b_qkv', 'w_proj', 'b_proj', 'rel_pos_h', 'rel_pos_w', )}
    del _L3_conv_all

    return {
        "x": x,
        "L0_conv_w_qkv": _L0_conv_in["w_qkv"],
        "L0_conv_w_out": _L0_conv_in["w_out"],
        "L1_conv_qkv_w": _L1_conv_in["qkv_w"],
        "L1_conv_qkv_b": _L1_conv_in["qkv_b"],
        "L1_conv_proj_w": _L1_conv_in["proj_w"],
        "L1_conv_proj_b": _L1_conv_in["proj_b"],
        "L1_conv_rel_pos_h": _L1_conv_in["rel_pos_h"],
        "L1_conv_rel_pos_w": _L1_conv_in["rel_pos_w"],
        "L2_conv_qkv_w": _L2_conv_in["qkv_w"],
        "L2_conv_qkv_b": _L2_conv_in["qkv_b"],
        "L2_conv_proj_w": _L2_conv_in["proj_w"],
        "L2_conv_proj_b": _L2_conv_in["proj_b"],
        "L3_conv_w_qkv": _L3_conv_in["w_qkv"],
        "L3_conv_b_qkv": _L3_conv_in["b_qkv"],
        "L3_conv_w_proj": _L3_conv_in["w_proj"],
        "L3_conv_b_proj": _L3_conv_in["b_proj"],
        "L3_conv_rel_pos_h": _L3_conv_in["rel_pos_h"],
        "L3_conv_rel_pos_w": _L3_conv_in["rel_pos_w"],
    }

def reference(x, L0_conv_w_qkv, L0_conv_w_out, L1_conv_qkv_w, L1_conv_qkv_b, L1_conv_proj_w, L1_conv_proj_b, L1_conv_rel_pos_h, L1_conv_rel_pos_w, L2_conv_qkv_w, L2_conv_qkv_b, L2_conv_proj_w, L2_conv_proj_b, L3_conv_w_qkv, L3_conv_b_qkv, L3_conv_w_proj, L3_conv_b_proj, L3_conv_rel_pos_h, L3_conv_rel_pos_w):
    import jax
    import jax.numpy as jnp
    def _L0_conv_ref(x, w_qkv, w_out):
        import jax, jax.numpy as jnp
        import numpy as np
        D_HEAD = 64
        KV_GROUPS = 3
        KSIZE = 7

        def _win_idx(L, ksize):
            start = jnp.clip(jnp.arange(L) - ksize // 2, 0, L - ksize)
            return start[:, None] + jnp.arange(ksize)[None, :]

        def _natten2d(q, k, v, ksize):
            H, W = (q.shape[2], q.shape[3])
            ih = _win_idx(H, ksize)
            iw = _win_idx(W, ksize)
            kg = k[:, :, ih[:, None, :, None], iw[None, :, None, :], :]
            vg = v[:, :, ih[:, None, :, None], iw[None, :, None, :], :]
            logits = jnp.einsum('nhije,nhijabe->nhijab', q, kg)
            n_, nh = logits.shape[:2]
            a = jax.nn.softmax(logits.reshape(n_, nh, H, W, ksize * ksize), axis=-1)
            a = a.reshape(logits.shape)
            return jnp.einsum('nhijab,nhijabe->nhije', a, vg)

        def _to_heads(p, nh, e):
            n, h, w, _ = p.shape
            return p.reshape(n, h, w, nh, e).transpose(0, 3, 1, 2, 4)
        n, H, W, d_model = x.shape
        q_heads = d_model // D_HEAD
        kv_heads = q_heads // KV_GROUPS
        qkv = x @ w_qkv.T
        q, k, v = jnp.split(qkv, [q_heads * D_HEAD, (q_heads + kv_heads) * D_HEAD], axis=-1)
        q = _to_heads(q, q_heads, D_HEAD)
        k = jnp.tile(_to_heads(k, kv_heads, D_HEAD), (1, KV_GROUPS, 1, 1, 1))
        v = jnp.tile(_to_heads(v, kv_heads, D_HEAD), (1, KV_GROUPS, 1, 1, 1))
        q = q / D_HEAD ** 0.5
        o = _natten2d(q, k, v, KSIZE)
        o = o.transpose(0, 2, 3, 1, 4).reshape(n, H, W, d_model)
        return o @ w_out.T

    def _L1_conv_ref(x, qkv_w, qkv_b, proj_w, proj_b, rel_pos_h, rel_pos_w):
        import jax, jax.numpy as jnp
        import numpy as np
        NUM_HEADS = 12
        H = W = 64
        DIM = 768
        HEAD_DIM = DIM // NUM_HEADS

        def _get_rel_pos(size: int, rel_pos: jnp.ndarray) -> jnp.ndarray:
            coords = jnp.arange(size)[:, None] - jnp.arange(size)[None, :] + (size - 1)
            return rel_pos[coords]
        B, h, w, C = x.shape
        nh, hd = (NUM_HEADS, C // NUM_HEADS)
        S = h * w
        scale = hd ** (-0.5)
        qkv = x.reshape(B, S, C) @ qkv_w.T + qkv_b
        qkv = qkv.reshape(B, S, 3, nh, hd).transpose(2, 0, 3, 1, 4)
        qkv = qkv.reshape(3, B * nh, S, hd)
        q, k, v = (qkv[0], qkv[1], qkv[2])
        attn = jnp.einsum('bqc,bkc->bqk', q * scale, k)
        Rh = _get_rel_pos(h, rel_pos_h)
        Rw = _get_rel_pos(w, rel_pos_w)
        r_q = q.reshape(B * nh, h, w, hd)
        rel_h = jnp.einsum('bhwc,hkc->bhwk', r_q, Rh)
        rel_w = jnp.einsum('bhwc,wkc->bhwk', r_q, Rw)
        attn = (attn.reshape(B * nh, h, w, h, w) + rel_h[:, :, :, :, None] + rel_w[:, :, :, None, :]).reshape(B * nh, S, S)
        attn = jax.nn.softmax(attn, axis=-1)
        out = jnp.einsum('bqk,bkc->bqc', attn, v)
        out = out.reshape(B, nh, h, w, hd).transpose(0, 2, 3, 1, 4).reshape(B, h, w, C)
        return out @ proj_w.T + proj_b

    def _L2_conv_ref(x, qkv_w, qkv_b, proj_w, proj_b):
        import jax, jax.numpy as jnp
        import numpy as np
        NUM_HEADS = 12
        B, H, W, C = x.shape
        N = H * W
        nh = NUM_HEADS
        qkv = jnp.einsum('bhwc,dc->bhwd', x, qkv_w) + qkv_b
        qkv = qkv.reshape(B, N, 3, nh, -1)
        q, k, v = (qkv[:, :, 0], qkv[:, :, 1], qkv[:, :, 2])
        q = q.transpose(0, 2, 1, 3)
        k = k.transpose(0, 2, 1, 3)
        v = v.transpose(0, 2, 1, 3)
        hd = q.shape[-1]
        scale = hd ** (-0.5)
        scores = jnp.einsum('bhnd,bhmd->bhnm', q, k) * scale
        attn = jax.nn.softmax(scores.astype(jnp.float32), axis=-1).astype(q.dtype)
        attn = jax.lax.stop_gradient(attn)
        out = jnp.einsum('bhnm,bhmd->bhnd', attn, v)
        out = out.transpose(0, 2, 1, 3).reshape(B, H, W, -1)
        out = jnp.einsum('bhwc,dc->bhwd', out, proj_w) + proj_b
        return out

    def _L3_conv_ref(x, w_qkv, b_qkv, w_proj, b_proj, rel_pos_h, rel_pos_w, nb_heads):
        import jax, jax.numpy as jnp
        import numpy as np

        def _rel_pos_table(size, rel_pos):
            coords = jnp.arange(size)[:, None] - jnp.arange(size)[None, :] + (size - 1)
            return rel_pos[coords]
        N, H, W, C = x.shape
        hd = C // nb_heads
        scale = hd ** (-0.5)
        HW = H * W
        qkv = x.reshape(N, HW, C) @ w_qkv + b_qkv
        qkv = qkv.reshape(N, HW, 3, nb_heads, hd)
        qkv = jnp.transpose(qkv, (2, 0, 3, 1, 4)).reshape(3, N * nb_heads, HW, hd)
        q, k, v = (qkv[0], qkv[1], qkv[2])
        attn = jnp.einsum('bqd,bkd->bqk', q, k) * scale
        r_h = _rel_pos_table(H, rel_pos_h)
        r_w = _rel_pos_table(W, rel_pos_w)
        q4 = q.reshape(N * nb_heads, H, W, hd)
        bias_h = jnp.einsum('nhwc,hkc->nhwk', q4, r_h)
        bias_w = jnp.einsum('nhwc,wkc->nhwk', q4, r_w)
        attn = attn.reshape(N * nb_heads, H, W, H, W)
        attn = attn + bias_h[..., :, None] + bias_w[..., None, :]
        attn = attn.reshape(N * nb_heads, HW, HW)
        attn = jax.nn.softmax(attn, axis=-1)
        out = jnp.einsum('bqk,bkd->bqd', attn, v)
        out = out.reshape(N, nb_heads, H, W, hd)
        out = jnp.transpose(out, (0, 2, 3, 1, 4)).reshape(N, H, W, C)
        return out @ w_proj + b_proj

    def _gn(v, G=32, eps=1e-5):
        B_, H_, W_, C_ = v.shape
        g = v.reshape(B_, H_, W_, G, C_ // G)
        m = jnp.mean(g, axis=(1, 2, 4), keepdims=True)
        s = jnp.var(g, axis=(1, 2, 4), keepdims=True)
        return ((g - m) / jnp.sqrt(s + eps)).reshape(v.shape)

    def _ln_c(v, eps=1e-6):
        m = jnp.mean(v, axis=-1, keepdims=True)
        s = jnp.var(v, axis=-1, keepdims=True)
        return (v - m) / jnp.sqrt(s + eps)

    def _ln_t(v, eps=1e-5):
        m = jnp.mean(v, axis=-1, keepdims=True)
        s = jnp.var(v, axis=-1, keepdims=True)
        return (v - m) / jnp.sqrt(s + eps)

    def _to_tokens(v):
        B_, H_, W_, C_ = v.shape
        return v.reshape(B_, H_ * W_, C_)
    def _from_tokens(t, like):
        return t.reshape(like.shape)

    x = x + _L0_conv_ref(_gn(x), L0_conv_w_qkv, L0_conv_w_out)
    x = x + _L1_conv_ref(_gn(x), L1_conv_qkv_w, L1_conv_qkv_b, L1_conv_proj_w, L1_conv_proj_b, L1_conv_rel_pos_h, L1_conv_rel_pos_w)
    x = x + _L2_conv_ref(_gn(x), L2_conv_qkv_w, L2_conv_qkv_b, L2_conv_proj_w, L2_conv_proj_b)
    x = x + _L3_conv_ref(_gn(x), L3_conv_w_qkv, L3_conv_b_qkv, L3_conv_w_proj, L3_conv_b_proj, L3_conv_rel_pos_h, L3_conv_rel_pos_w, 12)
    return x


_drawn_inputs = setup_inputs


def setup_inputs(seed=0):
    import zlib

    import numpy as np

    out = dict(_drawn_inputs(seed))
    spreads = {'L2_conv_qkv_b': (0.0, 0.1), 'L2_conv_proj_b': (0.0, 0.1)}
    factors = {'L1_conv_qkv_b': 3.508,
     'L1_conv_rel_pos_h': 8.0,
     'L1_conv_rel_pos_w': 8.0,
     'L3_conv_b_qkv': 5.841,
     'L3_conv_b_proj': 3.042,
     'L3_conv_rel_pos_h': 49.71,
     'L3_conv_rel_pos_w': 50.122}
    for name, (base, spread) in spreads.items():
        noise = np.random.default_rng([zlib.crc32(name.encode()), seed]).standard_normal(out[name].shape)
        drawn = base * np.exp(spread * noise) if base else spread * noise
        out[name] = jnp.asarray(drawn.astype(out[name].dtype))
    for name, factor in factors.items():
        out[name] = (out[name] * factor).astype(out[name].dtype)
    return out
```

```python
from contextlib import ExitStack

import concourse.bass as bass
from concourse import mybir

F32 = mybir.dt.float32
F32R = mybir.dt.float32r
ALU = mybir.AluOpType
ACT = mybir.ActivationFunctionType
AX = mybir.AxisListType

P = 128
SIDE = 32
TOK = SIDE * SIDE
IMAGES = 2
C = 768
CH = C // P
D = 64
PAIRS = C // (2 * D)
KV_PAIRS0 = 2
GROUPS = 32
PER_GROUP = C // GROUPS
HALF = 512
QT = TOK // P
REL = 2 * SIDE - 1
RPL = 4
KSIZE = 7
GN_EPS = 1e-5
MASKED = -float(2.0 ** 60)
LAYERS = 4


def near(t):
    return max(t - 1, 0), min(t + 1, QT - 1) + 1


def steps(kind):
    if kind == 0:
        return [(kt, near(kt)[0] * P, near(kt)[1] * P) for kt in range(QT)]
    return [(kt, q, q + HALF) for kt in range(QT) for q in (0, HALF)]


def value_parts(kind, n):
    kt, lo, hi = steps(kind)[n]
    cuts = [(a, b) for a, b in ((lo, min(hi, HALF)), (max(lo, HALF), hi)) if a < b]
    before = steps(kind)[:n]
    return [(a, b, not any(s[1] < (a // HALF + 1) * HALF and s[2] > a // HALF * HALF for s in before))
            for a, b in cuts]


KV = (KV_PAIRS0, PAIRS)
STEPS = (len(steps(0)), len(steps(1)))
HEADS = 2 * PAIRS
GN_STEPS = 15
RAISED = {
    "params_in": (16 * 2, 16 * 2), "mask_in": (16, 0),
    "wq_in0": (16 * 6, 16 * 10), "wq_in1": (16 * 6, 16 * 10),
    "wk_in": (16 * KV[0], 16 * KV[1]), "wv_in": (16 * KV[0], 16 * KV[1]),
    "gn_dve": (GN_STEPS, GN_STEPS), "gn_pe": (4, 4), "gn_act": (1, 1), "xn_ready": (1, 1),
    "q_ps": (12, 12), "q_act0": (6, 6), "q_act1": (6, 6), "q_dve0": (6, 6), "q_dve1": (6, 6), "bk_ready": (1, 1),
    "relh_ps": (0, 16), "relw_ps": (0, 16), "relh_done": (0, 16), "relw_done": (0, 16),
    "k_ps": (2 * KV[0], 2 * KV[1]), "k_act": (2 * KV[0], 2 * KV[1]), "k_dve": (2 * KV[0], 2 * KV[1]),
    "v_ps": (2 * KV[0], 2 * KV[1]), "v_done": (2 * KV[0], 2 * KV[1]),
    "qr_ready": (HEADS, HEADS), "max_ps": (QT * HEADS, QT * HEADS), "max_done": (QT * HEADS, QT * HEADS),
    "diag_ready": (2 * HEADS, 2 * HEADS), "shift_ps": (2 * HEADS, 2 * HEADS), "shifted": (HEADS, HEADS),
    "score_ps": (HEADS * STEPS[0], HEADS * STEPS[1]), "exp_done": (HEADS * STEPS[0], HEADS * STEPS[1]),
    "value_ps": (HEADS * STEPS[0], HEADS * STEPS[1]), "o_act": (HEADS, HEADS), "sum_dve": (HEADS, HEADS),
    "recip_done": (4 * PAIRS, 4 * PAIRS), "norm_done": (4 * PAIRS, 4 * PAIRS),
    "proj_ps": (12, 12), "added0": (6, 6), "added1": (6, 6),
}
LIFTED = {"pe": ("k_ps", "v_ps", "proj_ps", "shift_ps"), "act": ("q_act0", "q_act1", "o_act"),
          "dve": ("q_dve0", "q_dve1", "sum_dve", "added0", "added1")}
START = {name: 1 for names in LIFTED.values() for name in names}
NP = 3


class Unit:

    def __init__(self, kind, n, image, layer):
        self.kind, self.n, self.image, self.layer = kind, n, image, layer

    def at(self, name, local):
        first = START.get(name, 0) + (IMAGES * RAISED[name][0] if self.kind else 0)
        return self.n * RAISED[name][self.kind] + (local + first)


def build(nc, xT_in, wq_in, wk_in, wv_in, wo_in, params_in, bv_in, rel_in, onehot_in, mask_in,
          ident_in, ind_in, indT_in, out):
    with ExitStack() as ctx:
        def sb(name, shape, dt=F32):
            return ctx.enter_context(nc.sbuf_tensor(name, shape, dt))

        def ps(name):
            return ctx.enter_context(nc.psum_tensor(name, [P, 2, HALF], F32))

        xT = sb("xT", [P, CH, IMAGES * TOK])
        xn = sb("xn", [P, CH, TOK])
        qop = sb("qop", [P, HEADS, TOK])
        qo = sb("qo", [P, PAIRS, TOK])
        kop = sb("kop", [P, 2, TOK])
        kr = sb("kr", [P, 2, TOK], F32R)
        qr = sb("qr", [P, TOK], F32R)
        vop = sb("vop", [P, QT, 2, P])
        probs = sb("probs", [P, NP, HALF])
        diag = sb("diag", [P, 2, HALF], F32R)
        wq = sb("wq", [P, 2, CH, P])
        wk = sb("wk", [P, CH, P])
        wv = sb("wv", [P, CH, P])
        par = sb("par", [P, 3, CH])
        bk8 = sb("bk8", [P, PAIRS])
        bv = sb("bv", [P, C])
        ident = sb("ident", [P, P])
        ones = sb("ones", [P, P], F32R)
        ind = sb("ind", [P, CH, GROUPS])
        indT = sb("indT", [GROUPS, C])
        negmax = sb("negmax", [P, 2, QT])
        bst = sb("bst", [P, CH, 2, 6])
        mv = sb("mv", [P, CH, 2])
        gsum = sb("gsum", [GROUPS, 2])
        cmean = sb("cmean", [P, CH])
        dev = sb("dev", [P, CH])
        var = sb("var", [P, CH])
        root = sb("root", [P, CH])
        rstd = sb("rstd", [P, CH])
        newt = sb("newt", [P, CH])
        nshift = sb("nshift", [P, CH])

        maxb, scb, pvb, pjb = ps("maxb"), ps("scb"), ps("pvb"), ps("pjb")

        S = {name: ctx.enter_context(nc.semaphore(name)) for name in RAISED}
        const_in = ctx.enter_context(nc.semaphore("const_in"))
        const_done = ctx.enter_context(nc.semaphore("const_done"))
        x_in = ctx.enter_context(nc.semaphore("x_in"))
        out_done = ctx.enter_context(nc.semaphore("out_done"))
        passed = ctx.enter_context(nc.semaphore("passed"))
        block = ctx.enter_context(nc.Block())

        def rel_tables(slot):
            flat = wq[:, slot].rearrange("p c o -> p (c o)")[:, 0:2 * RPL * D]
            return flat.rearrange("p (a r k) -> p a r k", a=2, r=RPL)

        def units(eng, body):
            with eng.Fori(0, IMAGES) as b:
                body(Unit(0, b, b, 0))
            with eng.Fori(0, LAYERS - 1) as layer:
                with eng.Fori(0, IMAGES) as b:
                    body(Unit(1, layer * IMAGES + b, b, layer + 1))

        def pairs_of(eng, kind, kv_body, pair_body):
            if kind == 0:
                with eng.Fori(0, KV_PAIRS0) as g:
                    kv_body(g)
                    with eng.Fori(0, PAIRS // KV_PAIRS0) as i:
                        pair_body(g * (PAIRS // KV_PAIRS0) + i, i * KV_PAIRS0 + g)
            else:
                with eng.Fori(0, PAIRS) as p:
                    kv_body(p)
                    pair_body(p, p)

        @block.sync
        def _(sp):
            for dst, src in ((ident[:], ident_in), (ind[:], ind_in), (indT[:], indT_in),
                             (kop[D:P, 0, :], onehot_in), (kop[D:P, 1, :], onehot_in)):
                sp.dma_start(dst, src).then_inc(const_in, 16)
            for b in range(IMAGES):
                for c in range(CH):
                    sp.dma_start(xT[:, c, b * TOK:(b + 1) * TOK],
                                 xT_in[c * P:(c + 1) * P, b * TOK:(b + 1) * TOK]).then_inc(x_in, 16)

            def unit(u):
                for h in range(2):
                    sp.wait_ge(S[f"added{h}"], u.at(f"added{h}", 0))
                sp.dma_start(par[:], params_in[u.layer]).then_inc(S["params_in"], 16)
                sp.dma_start(bv[:], bv_in[u.layer].partition_broadcast(P)).then_inc(S["params_in"], 16)
                if u.kind == 0:
                    for_all = mask_in.unsqueeze(1).to_broadcast([D, HEADS, TOK])
                    sp.dma_start(qop[D:P, :, :], for_all).then_inc(S["mask_in"], 16)

                def in_twos(src, used, before, all_before):
                    for slot in range(2):
                        sp.wait_ge(S[before], u.at(before, all_before))
                        sp.dma_start(wq[:, slot], src[u.layer, slot]).then_inc(S[f"wq_in{slot}"], 16)
                    with sp.Fori(1, PAIRS // 2) as i:
                        for slot in range(2):
                            sp.wait_ge(S[used], u.at(used, i * 4 + (2 * slot - 2)))
                            sp.dma_start(wq[:, slot], src[u.layer, i * 2 + slot]).then_inc(S[f"wq_in{slot}"], 16)

                in_twos(wq_in, "q_ps", "proj_ps", 0)
                if u.kind:
                    for n in range(SIDE // RPL):
                        if n < 2:
                            sp.wait_ge(S["q_ps"], u.at("q_ps", 12))
                        else:
                            sp.wait_ge(S["relw_ps"], u.at("relw_ps", 2 * n - 2))
                        sp.dma_start(rel_tables(n % 2), rel_in[u.layer - 1, n]).then_inc(S[f"wq_in{n % 2}"], 16)
                with sp.Fori(0, KV[u.kind]) as n:
                    sp.wait_ge(S["k_ps"], u.at("k_ps", n * 2))
                    sp.dma_start(wk[:], wk_in[u.layer, n]).then_inc(S["wk_in"], 16)
                    sp.wait_ge(S["v_ps"], u.at("v_ps", n * 2))
                    sp.dma_start(wv[:], wv_in[u.layer, n]).then_inc(S["wv_in"], 16)
                in_twos(wo_in, "proj_ps", *(("relw_ps", SIDE // 2) if u.kind else ("q_ps", 12)))

            units(sp, unit)
            for h in range(2):
                sp.wait_ge(S[f"added{h}"], START[f"added{h}"] + 6 * LAYERS * IMAGES)
            for c in range(CH):
                sp.dma_start(out[c * P:(c + 1) * P, :], xT[:, c, :]).then_inc(out_done, 16)
            sp.wait_ge(out_done, 16 * CH)

        @block.tensor
        def _(pe):
            for name in LIFTED["pe"]:
                pe.sem_inc(S[name], 1)
            pe.wait_ge(const_in, 16 * 5)
            pe.wait_ge(const_done, 3)

            def groups(u, base, rhs, step):
                pe.wait_ge(S["gn_dve"], u.at("gn_dve", step))
                for c in range(CH):
                    mm = pe.matmul(pjb[0:GROUPS, 0, 0:1], ind[:, c, :], rhs(c), start=(c == 0), stop=(c == CH - 1))
                mm.then_inc(S["gn_pe"], 1)
                pe.wait_ge(S["gn_dve"], u.at("gn_dve", step + 1))
                for c in range(CH):
                    mm = pe.matmul(pjb[:, 1, c:c + 1], indT[:, c * P:(c + 1) * P], gsum[:, base:base + 1],
                                   start=True, stop=True)
                mm.then_inc(S["gn_pe"], 1)

            def project(u, first, rhs, done, freed):
                with pe.Fori(0, PAIRS // 2) as i:
                    for slot in range(2):
                        pe.wait_ge(S[f"wq_in{slot}"], u.at(f"wq_in{slot}", i * 16 + (first + 1) * 16))
                        for h in range(2):
                            freed(h, i * 2 + slot)
                            for c in range(CH):
                                mm = pe.matmul(pjb[:, h, :], wq[:, slot, c, :], rhs(c, h),
                                               start=(c == 0), stop=(c == CH - 1))
                            mm.then_inc(S[done], 1)

            def unit(u):
                groups(u, 0, lambda c: mv[:, c, 0:1], 2)
                groups(u, 1, lambda c: dev[:, c:c + 1], 7)
                pe.wait_ge(S["xn_ready"], u.at("xn_ready", 1))
                pe.sem_inc(passed, 1)

                def q_freed(h, n):
                    pe.wait_ge(S[f"q_act{h}"], u.at(f"q_act{h}", n))
                    pe.wait_ge(S[f"q_dve{h}"], u.at(f"q_dve{h}", n))

                project(u, 0, lambda c, h: xn[:, c, h * HALF:(h + 1) * HALF], "q_ps", q_freed)

                for h in range(2):
                    q_freed(h, PAIRS)
                pe.sem_inc(passed, 1)
                if u.kind:
                    rows = qo[:].rearrange("p n (h w) -> p n h w", w=SIDE)
                    for g in range(SIDE // 2):
                        slot = g // 2 % 2
                        if g % 2 == 0:
                            pe.wait_ge(S[f"wq_in{slot}"], u.at(f"wq_in{slot}", 16 * (3 + g // 4 + 1)))
                        if g >= 2:
                            pe.wait_ge(S["relh_done"], u.at("relh_done", g - 1))
                        for i in range(2):
                            r = 2 * g + i
                            mm = pe.matmul(scb[0:D, g % 2, i * 192:(i + 1) * 192],
                                           rel_tables(slot)[:, 0, r % RPL, :], rows[:, :, r, :],
                                           start=True, stop=True)
                        mm.then_inc(S["relh_ps"], 1)
                        if g >= 2:
                            pe.wait_ge(S["relw_done"], u.at("relw_done", g - 1))
                        for i in range(2):
                            r = 2 * g + i
                            mm = pe.matmul(maxb[D:P, g % 2, i * 192:(i + 1) * 192],
                                           rel_tables(slot)[:, 1, r % RPL, :], rows[:, :, :, r],
                                           start=True, stop=True)
                        mm.then_inc(S["relw_ps"], 1)
                    pe.wait_ge(S["relh_done"], u.at("relh_done", 16))
                    pe.wait_ge(S["relw_done"], u.at("relw_done", 16))
                    pe.sem_inc(passed, 1)

                def k_proj(n):
                    pe.wait_ge(S["wk_in"], u.at("wk_in", n * 16 + 16))
                    for h in range(2):
                        for c in range(CH):
                            mm = pe.matmul(pjb[:, h, :], wk[:, c, :], xn[:, c, h * HALF:(h + 1) * HALF],
                                           start=(c == 0), stop=(c == CH - 1))
                        mm.then_inc(S["k_ps"], 1)

                def v_tile(n, t):
                    if t == 0:
                        pe.wait_ge(S["wv_in"], u.at("wv_in", n * 16 + 16))
                    for c in range(CH):
                        mm = pe.matmul(scb[:, t // 4, t % 4 * P:(t % 4 + 1) * P], xn[:, c, t * P:(t + 1) * P],
                                       wv[:, c, :], start=(c == 0), stop=(c == CH - 1))
                    if t % 4 == 3:
                        mm.then_inc(S["v_ps"], 1)

                def max_tile(head, e, t):
                    if t == 0:
                        pe.wait_ge(S["qr_ready"], u.at("qr_ready", head + 1))
                    if u.kind == 0:
                        if t >= 2:
                            pe.wait_ge(S["max_done"], u.at("max_done", head * QT + (t - 1)))
                        lo, hi = near(t)
                        mm = pe.matmul(maxb[:, t % 2, 0:(hi - lo) * P], qr[:, t * P:(t + 1) * P],
                                       kr[:, e, lo * P:hi * P], start=True, stop=True)
                    else:
                        if t >= 1:
                            pe.wait_ge(S["max_done"], u.at("max_done", head * QT + t))
                        for h in range(2):
                            mm = pe.matmul(maxb[:, h, :], qr[:, t * P:(t + 1) * P],
                                           kr[:, e, h * HALF:(h + 1) * HALF], start=True, stop=True)
                    mm.then_inc(S["max_ps"], 1)

                def shift(head):
                    for h in range(2):
                        pe.wait_ge(S["diag_ready"], u.at("diag_ready", head * 2 + h + 1))
                        if h == 0:
                            pe.wait_ge(S["max_done"], u.at("max_done", head * QT + QT))
                        pe.matmul(maxb[:, h, :], ones[:], diag[:, h, :], start=True, stop=True) \
                            .then_inc(S["shift_ps"], 1)

                def values(head, e, n):
                    pe.wait_ge(S["exp_done"], u.at("exp_done", head * STEPS[u.kind] + n + 1))
                    if n == 0:
                        pe.wait_ge(S["o_act"], u.at("o_act", head))
                        pe.wait_ge(S["sum_dve"], u.at("sum_dve", head))
                    kt, lo, _ = steps(u.kind)[n]
                    for a, b, first in value_parts(u.kind, n):
                        mm = pe.matmul(pvb[:, a // HALF, a % HALF:(b - 1) % HALF + 1], vop[:, kt, e, :],
                                       probs[:, n % NP, a - lo:b - lo], start=first, stop=True,
                                       skip_group_check=True)
                    mm.then_inc(S["value_ps"], 1)

                def attend(head, e, pair, beside):
                    pe.wait_ge(S["shifted"], u.at("shifted", head + 1))
                    for n, (kt, lo, hi) in enumerate(steps(u.kind)):
                        if n >= 2:
                            pe.wait_ge(S["exp_done"], u.at("exp_done", head * STEPS[u.kind] + (n - 1)))
                        pe.matmul(scb[:, n % 2, 0:hi - lo], kop[:, e, kt * P:(kt + 1) * P],
                                  qop[:, pair * 2 + e, lo:hi], start=True, stop=True) \
                            .then_inc(S["score_ps"], 1)
                        if n:
                            values(head, e, n - 1)
                        beside(n)
                    values(head, e, STEPS[u.kind] - 1)

                def kv(n):
                    k_proj(n)
                    for t in range(2 if u.kind else QT):
                        v_tile(n, t)
                    for h in range(2):
                        pe.wait_ge(S["k_act"], u.at("k_act", n * 2 + h + 1))
                        pe.wait_ge(S["k_dve"], u.at("k_dve", n * 2 + h + 1))
                    if u.kind == 0:
                        pe.wait_ge(S["v_done"], u.at("v_done", n * 2 + 2))
                    pe.sem_inc(passed, 1)

                def pair(n, p):
                    for t in range(QT):
                        max_tile(n * 2, 0, t)
                        if u.kind and t + 2 < QT:
                            v_tile(n, t + 2)
                    shift(n * 2)
                    if u.kind:
                        pe.wait_ge(S["v_done"], u.at("v_done", n * 2 + 2))

                    def next_head(step):
                        if step < QT:
                            max_tile(n * 2 + 1, 1, step)
                        elif step == QT + 3:
                            shift(n * 2 + 1)

                    attend(n * 2, 0, p, next_head)
                    if u.kind == 0:
                        shift(n * 2 + 1)
                    attend(n * 2 + 1, 1, p, lambda step: None)

                pairs_of(pe, u.kind, kv, pair)

                pe.wait_ge(S["norm_done"], u.at("norm_done", 4 * PAIRS))
                pe.sem_inc(passed, 1)

                def p_freed(h, n):
                    pe.wait_ge(S[f"added{h}"], u.at(f"added{h}", n))

                project(u, RAISED["wq_in0"][u.kind] // 16 - 3, lambda c, h: qo[:, c, h * HALF:(h + 1) * HALF], "proj_ps", p_freed)

            units(pe, unit)

        @block.scalar
        def _(act):
            for name in LIFTED["act"]:
                act.sem_inc(S[name], 1)

            def unit(u):
                act.wait_ge(S["gn_dve"], u.at("gn_dve", 9))
                act.activation(root[:], var[:], ACT.Sqrt).then_inc(S["gn_act"], 1)
                act.wait_ge(S["params_in"], u.at("params_in", RAISED["params_in"][u.kind]))
                with act.Fori(0, PAIRS) as p:
                    for h in range(2):
                        act.wait_ge(S["q_ps"], u.at("q_ps", p * 2 + h + 1))
                        act.sem_inc(passed, 1)
                        src, cols = pjb[0:D, h, :], slice(h * HALF, (h + 1) * HALF)
                        if u.kind:
                            act.activation(qo[0:D, p, cols], src, ACT.Identity, bias=par[0:D, 0, bass.ds(p, 1)])
                        act.activation(qop[0:D, p * 2, cols], src, ACT.Identity,
                                       bias=par[0:D, 0, bass.ds(p, 1)]).then_inc(S[f"q_act{h}"], 1)
                act.wait_ge(S["bk_ready"], u.at("bk_ready", 1))
                if u.kind:
                    heads = qop[:].rearrange("r (p e) (h w) -> r p e h w", e=2, w=SIDE)
                    for g in range(SIDE // 2):
                        act.wait_ge(S["relh_ps"], u.at("relh_ps", g + 1))
                        for e in range(2):
                            src = scb[e * SIDE:(e + 1) * SIDE, g % 2, 0:2 * 192].rearrange(
                                "k (i p w) -> k i p w", i=2, w=SIDE)
                            dst = heads[D:D + SIDE, :, e, 2 * g:2 * g + 2, :].rearrange("k p i w -> k i p w")
                            a = act.activation(dst, src, ACT.Copy)
                        a.then_inc(S["relh_done"], 1)

                def kv(n):
                    for h in range(2):
                        act.wait_ge(S["k_ps"], u.at("k_ps", n * 2 + h + 1))
                        act.sem_inc(passed, 1)
                        src, cols = pjb[0:D, h, :], slice(h * HALF, (h + 1) * HALF)
                        act.activation(kr[0:D, 0, cols], src, ACT.Identity, bias=bk8[0:D, bass.ds(n, 1)], scale=0.125)
                        act.activation(kop[0:D, 0, cols], src, ACT.Identity, bias=bk8[0:D, bass.ds(n, 1)],
                                       scale=0.125).then_inc(S["k_act"], 1)

                def pair(n, p):
                    for e in range(2):
                        for s, (kt, lo, hi) in enumerate(steps(u.kind)):
                            done = (n * 2 + e) * STEPS[u.kind] + s
                            act.wait_ge(S["score_ps"], u.at("score_ps", done + 1))
                            if s >= NP:
                                act.wait_ge(S["value_ps"], u.at("value_ps", done - (NP - 1)))
                            act.activation(probs[:, s % NP, 0:hi - lo], scb[:, s % 2, 0:hi - lo],
                                           ACT.Exp).then_inc(S["exp_done"], 1)
                        act.wait_ge(S["value_ps"], u.at("value_ps", (n * 2 + e + 1) * STEPS[u.kind]))
                        act.sem_inc(passed, 1)
                        act.activation(qo[e * D:(e + 1) * D, p, :].rearrange("p (a b) -> p a b", a=2),
                                       pvb[0:D, :, :], ACT.Copy).then_inc(S["o_act"], 1)

                pairs_of(act, u.kind, kv, pair)

            units(act, unit)

        @block.vector
        def _(dve):
            for name in LIFTED["dve"]:
                dve.sem_inc(S[name], 1)
            dve.memset(vop[:], 1.0).then_inc(const_done, 1)
            dve.wait_ge(const_in, 16 * 5)
            dve.tensor_copy(kr[D:P, :, :], kop[D:P, :, :]).then_inc(const_done, 1)
            dve.wait_ge(const_done, 2)
            dve.tensor_copy(ones[:], vop[:, 0, 0, :]).then_inc(const_done, 1)
            dve.wait_ge(const_done, 3)
            dve.wait_ge(x_in, 16 * CH * IMAGES)

            def unit(u):
                b0 = u.image * TOK

                def did(ins, step):
                    ins.then_inc(S["gn_dve"], 1)
                    dve.wait_ge(S["gn_dve"], u.at("gn_dve", step))
                    dve.sem_inc(passed, 1)

                for h in range(2):
                    dve.wait_ge(S[f"added{h}"], u.at(f"added{h}", 0))
                for c in range(CH):
                    for h in range(2):
                        a = dve.bn_stats(bst[:, c, h, :], xT[:, c, bass.ds(b0 + h * HALF, HALF)])
                did(a, 1)
                for c in range(CH):
                    a = dve.bn_aggr(mv[:, c, :], bst[:, c].rearrange("p a b -> p (a b)"))
                did(a, 2)
                dve.wait_ge(S["gn_pe"], u.at("gn_pe", 1))
                did(dve.tensor_scalar(gsum[:, 0:1], pjb[0:GROUPS, 0, 0:1], 1.0 / PER_GROUP, None, ALU.mult), 3)
                dve.wait_ge(S["gn_pe"], u.at("gn_pe", 2))
                did(dve.tensor_copy(cmean[:], pjb[:, 1, 0:CH]), 4)
                did(dve.tensor_tensor(dev[:], mv[:, :, 0], cmean[:], ALU.subtract), 5)
                did(dve.tensor_tensor(dev[:], dev[:], dev[:], ALU.mult), 6)
                did(dve.tensor_tensor(dev[:], dev[:], mv[:, :, 1], ALU.add), 7)
                dve.wait_ge(S["gn_pe"], u.at("gn_pe", 3))
                did(dve.tensor_scalar(gsum[:, 1:2], pjb[0:GROUPS, 0, 0:1], 1.0 / PER_GROUP, None, ALU.mult), 8)
                dve.wait_ge(S["gn_pe"], u.at("gn_pe", 4))
                did(dve.tensor_scalar(var[:], pjb[:, 1, 0:CH], GN_EPS, None, ALU.add), 9)
                dve.wait_ge(S["gn_act"], u.at("gn_act", 1))
                did(dve.reciprocal(rstd[:], root[:]), 10)
                did(dve.tensor_tensor(newt[:], rstd[:], rstd[:], ALU.mult), 11)
                did(dve.tensor_tensor(newt[:], newt[:], var[:], ALU.mult), 12)
                did(dve.tensor_scalar(newt[:], newt[:], -0.5, 1.5, ALU.mult, ALU.add), 13)
                did(dve.tensor_tensor(rstd[:], rstd[:], newt[:], ALU.mult), 14)
                did(dve.scalar_tensor_tensor(nshift[:], cmean[:], -1.0, rstd[:], ALU.mult, ALU.mult), 15)
                for c in range(CH):
                    a = dve.tensor_scalar(xn[:, c, :], xT[:, c, bass.ds(b0, TOK)], rstd[:, c:c + 1],
                                          nshift[:, c:c + 1], ALU.mult, ALU.add)
                a.then_inc(S["xn_ready"], 1)

                dve.wait_ge(S["params_in"], u.at("params_in", RAISED["params_in"][u.kind]))
                dve.tensor_scalar(bk8[:], par[:, 1, :], 0.125, None, ALU.mult).then_inc(S["bk_ready"], 1)
                with dve.Fori(0, PAIRS) as p:
                    for h in range(2):
                        dve.wait_ge(S["q_ps"], u.at("q_ps", p * 2 + h + 1))
                        src, cols = pjb[D:P, h, :], slice(h * HALF, (h + 1) * HALF)
                        if u.kind:
                            dve.tensor_scalar(qo[D:P, p, cols], src, par[D:P, 0, bass.ds(p, 1)], None, ALU.add)
                        dve.tensor_scalar(qop[0:D, p * 2 + 1, cols], src, par[D:P, 0, bass.ds(p, 1)], None,
                                          ALU.add).then_inc(S[f"q_dve{h}"], 1)
                if u.kind:
                    heads = qop[:].rearrange("r (p e) (h w) -> r p e h w", e=2, w=SIDE)
                    for g in range(SIDE // 2):
                        dve.wait_ge(S["relw_ps"], u.at("relw_ps", g + 1))
                        for e in range(2):
                            src = maxb[D + e * SIDE:D + (e + 1) * SIDE, g % 2, 0:2 * 192].rearrange(
                                "k (i p h) -> k i p h", i=2, h=SIDE)
                            dst = heads[D + SIDE:P, :, e, :, 2 * g:2 * g + 2].rearrange("k p h i -> k i p h")
                            a = dve.tensor_copy(dst, src)
                        a.then_inc(S["relw_done"], 1)

                def k_read(n):
                    dve.wait_ge(S["bk_ready"], u.at("bk_ready", 1))
                    for h in range(2):
                        dve.wait_ge(S["k_ps"], u.at("k_ps", n * 2 + h + 1))
                        src, cols = pjb[D:P, h, :], slice(h * HALF, (h + 1) * HALF)
                        dve.tensor_scalar(kr[0:D, 1, cols], src, 0.125, bk8[D:P, bass.ds(n, 1)], ALU.mult, ALU.add)
                        dve.tensor_scalar(kop[0:D, 1, cols], src, 0.125, bk8[D:P, bass.ds(n, 1)], ALU.mult,
                                          ALU.add).then_inc(S["k_dve"], 1)

                def v_read(n, g):
                    dve.wait_ge(S["v_ps"], u.at("v_ps", n * 2 + g + 1))
                    bias = bv[:, bass.ds(n * P, P)].rearrange("p (e d) -> p e d", e=2).unsqueeze(1)
                    dve.tensor_tensor(vop[:, 4 * g:4 * g + 4, :, 0:D],
                                      scb[:, g, :].rearrange("p (t e d) -> p t e d", t=4, e=2),
                                      bias.to_broadcast([P, 4, 2, D]), ALU.add).then_inc(S["v_done"], 1)

                def round_q(head, e, p):
                    if e == 0:
                        for h in range(2):
                            dve.wait_ge(S[f"q_act{h}"], u.at(f"q_act{h}", PAIRS))
                            dve.wait_ge(S[f"q_dve{h}"], u.at(f"q_dve{h}", PAIRS))
                        if u.kind:
                            dve.wait_ge(S["relh_done"], u.at("relh_done", 16))
                            dve.wait_ge(S["relw_done"], u.at("relw_done", 16))
                        else:
                            dve.wait_ge(S["mask_in"], u.at("mask_in", 16))
                        dve.sem_inc(passed, 1)
                    dve.tensor_copy(qr[:], qop[:, p * 2 + e, :]).then_inc(S["qr_ready"], 1)

                def reduce(head, e, t):
                    dve.wait_ge(S["max_ps"], u.at("max_ps", head * QT + t + 1))
                    if u.kind == 0:
                        src = maxb[:, t % 2, 0:(near(t)[1] - near(t)[0]) * P]
                    else:
                        src = maxb[:].rearrange("p a b -> p (a b)")
                    dve.tensor_reduce(negmax[:, e, t:t + 1], src, AX.X, ALU.max, negate=True) \
                        .then_inc(S["max_done"], 1)

                def shift(head, e, p):
                    dve.wait_ge(S["shift_ps"], u.at("shift_ps", head * 2 + 2))
                    rows = qop[D:D + SIDE, p * 2 + e, :].rearrange("p (a b) -> p a b", a=2)
                    dve.tensor_tensor(rows, maxb[D:D + SIDE, :, :], rows, ALU.add).then_inc(S["shifted"], 1)

                def sums(head, e, p):
                    dve.wait_ge(S["value_ps"], u.at("value_ps", (head + 1) * STEPS[u.kind]))
                    dve.sem_inc(passed, 1)
                    dve.tensor_copy(qop[e * D:(e + 1) * D, p * 2, :].rearrange("p (a b) -> p a b", a=2),
                                    pvb[D:P, :, :]).then_inc(S["sum_dve"], 1)

                def divide(n, p, part):
                    if part == 0:
                        dve.wait_ge(S["sum_dve"], u.at("sum_dve", n * 2 + 2))
                        dve.wait_ge(S["o_act"], u.at("o_act", n * 2 + 2))
                        dve.sem_inc(passed, 1)
                    cols = slice(part * (TOK // 4), (part + 1) * (TOK // 4))
                    dve.reciprocal(qop[:, p * 2, cols], qop[:, p * 2, cols]).then_inc(S["recip_done"], 1)
                    dve.wait_ge(S["recip_done"], u.at("recip_done", n * 4 + part + 1))
                    dve.tensor_tensor(qo[:, p, cols], qo[:, p, cols], qop[:, p * 2, cols], ALU.mult) \
                        .then_inc(S["norm_done"], 1)

                def pair(n, p):
                    round_q(n * 2, 0, p)
                    for t in range(QT):
                        reduce(n * 2, 0, t)
                        if u.kind and t == 3:
                            v_read(n, 0)
                    if u.kind:
                        v_read(n, 1)
                    shift(n * 2, 0, p)
                    round_q(n * 2 + 1, 1, p)
                    for t in range(QT):
                        reduce(n * 2 + 1, 1, t)
                    shift(n * 2 + 1, 1, p)
                    sums(n * 2, 0, p)
                    sums(n * 2 + 1, 1, p)
                    for part in range(4):
                        divide(n, p, part)

                def kv(n):
                    k_read(n)
                    if u.kind == 0:
                        v_read(n, 0)
                        v_read(n, 1)

                pairs_of(dve, u.kind, kv, pair)

                with dve.Fori(0, CH) as c:
                    for h in range(2):
                        dve.wait_ge(S["proj_ps"], u.at("proj_ps", c * 2 + h + 1))
                        cols = bass.ds(b0 + h * HALF, HALF)
                        dve.scalar_tensor_tensor(xT[:, c, cols], pjb[:, h, :], par[:, 2, bass.ds(c, 1)],
                                                 xT[:, c, cols], ALU.add, ALU.add).then_inc(S[f"added{h}"], 1)

            units(dve, unit)

        @block.gpsimd
        def _(pool):
            pool.wait_ge(const_in, 16 * 5)

            def unit(u):
                def pair(n, p):
                    for e in range(2):
                        for h in range(2):
                            head = n * 2 + e
                            pool.wait_ge(S["max_done"], u.at("max_done", head * QT + 4 * h + 4))
                            pool.wait_ge(S["shift_ps"], u.at("shift_ps", head * 2))
                            pool.tensor_tensor(
                                diag[:, h, :].rearrange("p (t q) -> p t q", t=4),
                                ident[:].unsqueeze(1).to_broadcast([P, 4, P]),
                                negmax[:, e, 4 * h:4 * h + 4].unsqueeze(2).to_broadcast([P, 4, P]),
                                ALU.mult).then_inc(S["diag_ready"], 1)

                pairs_of(pool, u.kind, lambda n: None, pair)

            units(pool, unit)


_SHAPES = [("xT_in", (C, IMAGES * TOK)), ("wq_in", (LAYERS, PAIRS, P, CH, P)), ("wk_in", (LAYERS, PAIRS, P, CH, P)),
           ("wv_in", (LAYERS, PAIRS, P, CH, P)), ("wo_in", (LAYERS, PAIRS, P, CH, P)),
           ("params_in", (LAYERS, P, 3, CH)), ("bv_in", (LAYERS, C)), ("rel_in", (LAYERS - 1, SIDE // RPL, P, 2, RPL, D)),
           ("onehot_in", (2 * SIDE, TOK)), ("mask_in", (2 * SIDE, TOK)), ("ident_in", (P, P)),
           ("ind_in", (P, CH, GROUPS)), ("indT_in", (GROUPS, C))]


def lay_out(inputs):
    import numpy as np

    def blocks(w):
        n = w.shape[1] // P
        full = np.zeros((PAIRS, P, CH, P), np.float32)
        full[:n] = w.reshape(CH, P, n, P).transpose(2, 1, 0, 3)
        return full

    g = {k: np.asarray(v) for k, v in inputs.items()}
    kv0 = KV_PAIRS0 * P
    wT = [g["L0_conv_w_qkv"].T, g["L1_conv_qkv_w"].T, g["L2_conv_qkv_w"].T, g["L3_conv_w_qkv"]]
    cuts = [(C, C + kv0)] + [(C, 2 * C)] * 3
    zero = np.zeros((C,), np.float32)
    qkvb = [None, g["L1_conv_qkv_b"], g["L2_conv_qkv_b"], g["L3_conv_b_qkv"]]
    ob = [zero, g["L1_conv_proj_b"], g["L2_conv_proj_b"], g["L3_conv_b_proj"]]
    wo = [g["L0_conv_w_out"].T, g["L1_conv_proj_w"].T, g["L2_conv_proj_w"].T, g["L3_conv_w_proj"]]

    def bias(i, part):
        return zero if qkvb[i] is None else qkvb[i][part * C:(part + 1) * C]

    params = np.stack([np.stack([b.reshape(CH, P).T for b in (bias(i, 0), bias(i, 1), ob[i])], axis=1)
                       for i in range(LAYERS)])
    rel = np.zeros((LAYERS - 1, P, 2, SIDE, 2, SIDE), np.float32)
    which = np.arange(SIDE)[:, None] - np.arange(SIDE)[None] + SIDE - 1
    for i, layer in ((0, "L1"), (2, "L3")):
        for a, axis in enumerate(("h", "w")):
            table = g[f"{layer}_conv_rel_pos_{axis}"][which].transpose(2, 0, 1)
            rel[i, 0:D, a, :, 0] = table
            rel[i, D:P, a, :, 1] = table
    rel = rel.reshape(LAYERS - 1, P, 2, SIDE // RPL, RPL, D).transpose(0, 3, 1, 2, 4, 5)
    row, col = np.divmod(np.arange(TOK), SIDE)
    k = np.arange(SIDE)[:, None]

    def window(at):
        first = np.clip(at - KSIZE // 2, 0, SIDE - KSIZE)[None]
        return np.where((k >= first) & (k < first + KSIZE), 0.0, MASKED)

    group = np.arange(C) // PER_GROUP
    ind = (group[:, None] == np.arange(GROUPS)).astype(np.float32)
    return {
        "xT_in": g["x"].reshape(IMAGES * TOK, C).T,
        "wq_in": np.stack([blocks(w[:, :C]) for w in wT]),
        "wk_in": np.stack([blocks(w[:, a:b]) for w, (a, b) in zip(wT, cuts)]),
        "wv_in": np.stack([blocks(w[:, b:]) for w, (a, b) in zip(wT, cuts)]),
        "wo_in": np.stack([blocks(w) for w in wo]),
        "params_in": params,
        "bv_in": np.stack([bias(i, 2) for i in range(LAYERS)]),
        "rel_in": rel,
        "onehot_in": np.concatenate([k == row, k == col]).astype(np.float32),
        "mask_in": np.concatenate([window(row), window(col)]).astype(np.float32),
        "ident_in": np.eye(P, dtype=np.float32),
        "ind_in": ind.reshape(CH, P, GROUPS).transpose(1, 0, 2),
        "indT_in": ind.T,
    }


def kernel(**inputs):
    import numpy as np
    import concourse.bacc as bacc
    from concourse.bass_utils import run_bass_kernel_spmd

    nc = bacc.Bacc("TRN2", target_bir_lowering=False, num_devices=1)
    laid = lay_out(inputs)
    arrays, args = {}, {}
    for name, shape in _SHAPES:
        arrays[name] = np.ascontiguousarray(laid[name])
        assert arrays[name].shape == shape and arrays[name].dtype == np.float32, name
        args[name] = nc.dram_tensor(name, shape, F32, kind="ExternalInput").ap()
    out = nc.dram_tensor("out", (C, IMAGES * TOK), F32, kind="ExternalOutput").ap()
    build(nc, out=out, **args)
    r = run_bass_kernel_spmd(nc, [arrays], core_ids=[0])
    return np.ascontiguousarray(r.results[0]["out"].T).reshape(IMAGES, SIDE, SIDE, C)
```

```python
from contextlib import ExitStack

import concourse.bass as bass
from concourse import mybir

F32 = mybir.dt.float32
F32R = mybir.dt.float32r
ALU = mybir.AluOpType
ACT = mybir.ActivationFunctionType
AX = mybir.AxisListType

P = 128
SIDE = 32
TOK = SIDE * SIDE
IMAGES = 2
C = 768
CH = C // P
D = 64
PAIRS = C // (2 * D)
KV_PAIRS0 = 2
GROUPS = 32
PER_GROUP = C // GROUPS
HALF = 512
QT = TOK // P
REL = 2 * SIDE - 1
RPL = 4
KSIZE = 7
GN_EPS = 1e-5
MASKED = -float(2.0 ** 60)
LAYERS = 4


def near(t):
    return max(t - 1, 0), min(t + 1, QT - 1) + 1


def steps(kind):
    if kind == 0:
        return [(kt, near(kt)[0] * P, near(kt)[1] * P) for kt in range(QT)]
    return [(kt, q, q + HALF) for kt in range(QT) for q in (0, HALF)]


def value_parts(kind, n):
    kt, lo, hi = steps(kind)[n]
    cuts = [(a, b) for a, b in ((lo, min(hi, HALF)), (max(lo, HALF), hi)) if a < b]
    before = steps(kind)[:n]
    return [(a, b, not any(s[1] < (a // HALF + 1) * HALF and s[2] > a // HALF * HALF for s in before))
            for a, b in cuts]


class Places:

    def __init__(self, maxima, round_q, shift, qf, divide, k, k_read, v, v_read, diag):
        self.maxima = maxima
        self.round_q = round_q
        self.shift = shift
        self.qf = qf
        self.divide = divide
        self.k, self.k_read = k, k_read
        self.v, self.v_read = v, v_read
        self.diag = diag


PLACES = (
    Places(maxima=(0, 1, 1, 2, 3, 3, 4, 5), round_q=6, shift=7, qf=3, divide=((2, 4, 5, 6), (2, 4, 5, 6)),
           k=(), k_read=(), v=(), v_read=(), diag=(3, 6)),
    Places(maxima=(0, 1, 3, 4, 6, 8, 10, 11), round_q=12, shift=14, qf=8, divide=((2, 5, 7, 9), (2, 5, 8, 9)),
           k=(2, 3, 5, 7, 9, 12), k_read=(6, 13), v=(2, 3, 5, 6, 7, 9, 10, 12), v_read=(7, 13), diag=(5, 12)),
)
PARTS = 8

KV = (KV_PAIRS0, PAIRS)
STEPS = (len(steps(0)), len(steps(1)))
HEADS = 2 * PAIRS
GN_STEPS = 15
RAISED = {
    "params_in": (16 * 2, 16 * 2), "mask_in": (32, 0),
    "wq_in0": (16 * 6, 16 * 10), "wq_in1": (16 * 6, 16 * 10),
    "wk_in": (16 * KV[0], 16 * KV[1]), "wv_in": (16 * KV[0], 16 * KV[1]),
    "x_in": (16 * 6, 16 * 6), "xe_in0": (16 * 3, 16 * 3), "xe_in1": (16 * 3, 16 * 3),
    "stored0": (16 * 3, 16 * 3), "stored1": (16 * 3, 16 * 3),
    "gn_dve": (GN_STEPS, GN_STEPS), "gn_pe": (4, 4), "gn_act": (1, 1), "xn_ready": (1, 1),
    "q_ps": (12, 12), "q_act0": (6, 6), "q_act1": (6, 6), "q_dve0": (6, 6), "q_dve1": (6, 6), "bk_ready": (1, 1),
    "relh_ps": (0, 16), "relw_ps": (0, 16), "relh_done": (0, 16), "relw_done": (0, 16),
    "k_ps": (2 * KV[0], 2 * KV[1]), "k_act": (2 * KV[0], 2 * KV[1]), "k_dve": (2 * KV[0], 2 * KV[1]),
    "v_ps": (2 * KV[0], 2 * KV[1]), "v_done": (2 * KV[0], 2 * KV[1]),
    "qr_ready": (HEADS, HEADS), "max_ps": (QT * HEADS, QT * HEADS), "max_done": (QT * HEADS, QT * HEADS),
    "diag_ready": (2 * HEADS, 2 * HEADS), "shift_ps": (2 * HEADS, 2 * HEADS), "shifted": (HEADS, HEADS),
    "score_ps": (HEADS * STEPS[0], HEADS * STEPS[1]), "exp_done": (HEADS * STEPS[0], HEADS * STEPS[1]),
    "value_ps": (HEADS * STEPS[0], HEADS * STEPS[1]), "o_act": (HEADS, HEADS), "o_dve": (HEADS, HEADS), "sum_act": (HEADS, HEADS),
    "qf_act": (HEADS, HEADS), "high_done": (HEADS * STEPS[0], HEADS * STEPS[1]),
    "low_done": (HEADS * STEPS[0], HEADS * STEPS[1]),
    "tallied": (HEADS * STEPS[0], HEADS * (STEPS[1] - 2)), "sum_ps": (HEADS, HEADS),
    "v_step": (4 * KV[0], 4 * KV[1]), "recip_done": (8 * PAIRS, 8 * PAIRS), "norm_done": (8 * PAIRS, 8 * PAIRS),
    "proj_ps": (12, 12), "added0": (6, 6), "added1": (6, 6),
}
LIFTED = {"pe": ("k_ps", "v_ps", "proj_ps", "shift_ps", "sum_ps"), "act": ("q_act0", "q_act1", "o_act", "sum_act", "stored0", "stored1"),
          "dve": ("q_dve0", "q_dve1", "v_done", "o_dve", "added0", "added1")}
START = {name: 1 for names in LIFTED.values() for name in names}
START["proj_ps"] = 3
NP = 4
NR = 3
GN_BESIDE = (5, 6, 7, 8)
ROOT_AT = 4
GN_AFTER = (1, 3, 5, 6, 7, 8, 9)
TALLIES = tuple(RAISED["tallied"][k] // HEADS for k in range(2))


class Unit:

    def __init__(self, kind, n, image, layer):
        self.kind, self.n, self.image, self.layer = kind, n, image, layer

    def at(self, name, local):
        first = START.get(name, 0) + (IMAGES * RAISED[name][0] if self.kind else 0)
        return self.n * RAISED[name][self.kind] + (local + first)


def build(nc, xT_in, wq_in, wk_in, wv_in, wo_in, params_in, bv_in, rel_in, onehot_in, mask_in,
          ident_in, ind_in, indT_in, out):
    with ExitStack() as ctx:
        def sb(name, shape, dt=F32):
            return ctx.enter_context(nc.sbuf_tensor(name, shape, dt))

        def ps(name):
            return ctx.enter_context(nc.psum_tensor(name, [P, 2, HALF], F32))

        xn = sb("xn", [P, CH, TOK])
        xe = sb("xe", [P, 2, TOK])
        relp = sb("relp", [P, PAIRS, TOK])
        qf = sb("qf", [P, 2, TOK])
        qo = sb("qo", [P, PAIRS, TOK])
        kop = sb("kop", [P, 2, 2, TOK])
        kr = sb("kr", [P, 2, 2, TOK], F32R)
        qr = sb("qr", [P, TOK], F32R)
        vop = sb("vop", [P, 2, QT, 2, 2, D], F32R)
        vraw = sb("vraw", [P, 4, 2, D])
        probs = sb("probs", [P, NP, HALF])
        high = sb("high", [P, NR, HALF], F32R)
        low = sb("low", [P, NR, HALF], F32R)
        tally = sb("tally", [P, TOK])
        diag = sb("diag", [P, 2, HALF], F32R)
        wq = sb("wq", [P, 2, CH, P])
        wk = sb("wk", [P, CH, P])
        wv = sb("wv", [P, CH, P])
        par = sb("par", [P, 3, CH])
        bk8 = sb("bk8", [P, PAIRS])
        bv = sb("bv", [P, C])
        ident = sb("ident", [P, P])
        ones = sb("ones", [P, P])
        ones_r = sb("ones_r", [P, P], F32R)
        ind = sb("ind", [P, CH, GROUPS])
        indT = sb("indT", [GROUPS, C])
        negmax = sb("negmax", [P, 2, QT])
        bst = sb("bst", [P, CH, 2, 6])
        mv = sb("mv", [P, CH, 2])
        gsum = sb("gsum", [GROUPS, 2])
        cmean = sb("cmean", [P, CH])
        dev = sb("dev", [P, CH])
        var = sb("var", [P, CH])
        root = sb("root", [P, CH])
        rstd = sb("rstd", [P, CH])
        newt = sb("newt", [P, CH])
        nshift = sb("nshift", [P, CH])

        maxb, scb, pvb, pjb = ps("maxb"), ps("scb"), ps("pvb"), ps("pjb")

        S = {name: ctx.enter_context(nc.semaphore(name)) for name in RAISED}
        const_in = ctx.enter_context(nc.semaphore("const_in"))
        const_done = ctx.enter_context(nc.semaphore("const_done"))
        copied = ctx.enter_context(nc.semaphore("copied"))
        passed = ctx.enter_context(nc.semaphore("passed"))
        block = ctx.enter_context(nc.Block())

        def rel_tables(slot):
            flat = wq[:, slot].rearrange("p c o -> p (c o)")[:, 0:2 * RPL * D]
            return flat.rearrange("p (a r k) -> p a r k", a=2, r=RPL)

        def raw(kind, s):
            _, lo, hi = steps(kind)[s]
            return tally[:, lo:hi] if kind and s < 2 else probs[:, s % NP, 0:hi - lo]

        def units(eng, body):
            with eng.Fori(0, IMAGES) as b:
                body(Unit(0, b, b, 0))
            with eng.Fori(0, LAYERS - 1) as layer:
                with eng.Fori(0, IMAGES) as b:
                    body(Unit(1, layer * IMAGES + b, b, layer + 1))

        def pairs_of(eng, body):
            body(0, 0, False, True)
            with eng.Fori(0, (PAIRS - 2) // 2) as i:
                body(i * 2 + 1, 1, True, True)
                body(i * 2 + 2, 0, True, True)
            body(PAIRS - 1, 1, True, False)

        def of_next(u):
            return lambda name, local: u.at(name, local + RAISED[name][u.kind])

        @block.sync
        def _(sp):
            for c in range(CH):
                sp.dma_start(xn[:, c, :], xT_in[c * P:(c + 1) * P, 0:TOK]).then_inc(S["x_in"], 16)
            for dst, src in ((ident[:], ident_in), (ind[:], ind_in), (indT[:], indT_in)):
                sp.dma_start(dst, src).then_inc(const_in, 16)
            for parity in range(2):
                for e in range(2):
                    sp.dma_start(kop[D:P, parity, e, :], onehot_in).then_inc(const_in, 16)

            def unit(u):
                for slot in range(2):
                    sp.wait_ge(S["proj_ps"], u.at("proj_ps", 2 * slot - 2))
                    sp.dma_start(wq[:, slot], wq_in[u.layer, slot]).then_inc(S[f"wq_in{slot}"], 16)
                for h in range(2):
                    sp.wait_ge(S[f"added{h}"], u.at(f"added{h}", 0))
                sp.dma_start(par[:], params_in[u.layer]).then_inc(S["params_in"], 16)
                sp.dma_start(bv[:], bv_in[u.layer].partition_broadcast(P)).then_inc(S["params_in"], 16)
                if u.kind == 0:
                    for e in range(2):
                        for_all = mask_in.unsqueeze(1).to_broadcast([D, PAIRS, TOK])
                        sp.dma_start(relp[e * D:(e + 1) * D, :, :], for_all).then_inc(S["mask_in"], 16)
                with sp.Fori(1, PAIRS // 2) as i:
                    for slot in range(2):
                        sp.wait_ge(S["q_ps"], u.at("q_ps", i * 4 + (2 * slot - 2)))
                        sp.dma_start(wq[:, slot], wq_in[u.layer, i * 2 + slot]).then_inc(S[f"wq_in{slot}"], 16)

                def kv_weights(n):
                    sp.wait_ge(S["k_ps"], u.at("k_ps", n * 2))
                    sp.dma_start(wk[:], wk_in[u.layer, n]).then_inc(S["wk_in"], 16)
                    sp.wait_ge(S["v_ps"], u.at("v_ps", n * 2))
                    sp.dma_start(wv[:], wv_in[u.layer, n]).then_inc(S["wv_in"], 16)

                kv_weights(0)
                if u.kind:
                    for n in range(SIDE // RPL):
                        if n < 2:
                            sp.wait_ge(S["q_ps"], u.at("q_ps", 12))
                        else:
                            sp.wait_ge(S["relw_ps"], u.at("relw_ps", 2 * n - 2))
                        sp.dma_start(rel_tables(n % 2), rel_in[u.layer - 1, n]).then_inc(S[f"wq_in{n % 2}"], 16)
                with sp.Fori(1, KV[u.kind]) as n:
                    kv_weights(n)

                sp.wait_ge(S["k_ps"], u.at("k_ps", 2 * KV[u.kind]))
                sp.wait_ge(S["v_ps"], u.at("v_ps", 2 * KV[u.kind]))
                for h in range(2):
                    sp.wait_ge(S[f"stored{h}"], u.at(f"stored{h}", 0))
                sp.wait_ge(copied, 16 * CH)
                for c in range(CH):
                    sp.dma_start(xn[:, c, :], out[c * P:(c + 1) * P, bass.ds(u.image * -TOK + TOK, TOK)]) \
                        .then_inc(S["x_in"], 16)

                for c in range(CH):
                    slot = c % 2
                    if c < 2:
                        sp.wait_ge(*((S["relw_ps"], u.at("relw_ps", SIDE // 2)) if u.kind else
                                     (S["q_ps"], u.at("q_ps", 12))))
                    else:
                        sp.wait_ge(S["proj_ps"], u.at("proj_ps", 2 * c - 2))
                    sp.dma_start(wq[:, slot], wo_in[u.layer, c]).then_inc(S[f"wq_in{slot}"], 16)
                    sp.wait_ge(S[f"stored{slot}"], u.at(f"stored{slot}", 16 * (c // 2)))
                    sp.dma_start(xe[:, slot, :], out[c * P:(c + 1) * P, bass.ds(u.image * TOK, TOK)]) \
                        .then_inc(S[f"xe_in{slot}"], 16)

            units(sp, unit)
            for slot in range(2):
                sp.wait_ge(S[f"stored{slot}"], START[f"stored{slot}"] + 16 * 3 * LAYERS * IMAGES)
            sp.wait_ge(S["x_in"], 16 * 6 * (LAYERS * IMAGES + 1))

        @block.tensor
        def _(pe):
            for name in LIFTED["pe"]:
                pe.sem_inc(S[name], START[name])
            pe.wait_ge(const_in, 16 * 7)
            pe.wait_ge(const_done, 3)

            def gather(at, rhs, step):
                pe.wait_ge(S["gn_dve"], at("gn_dve", step))
                for c in range(CH):
                    mm = pe.matmul(maxb[0:GROUPS, 0, 0:1], ind[:, c, :], rhs(c), start=(c == 0), stop=(c == CH - 1))
                mm.then_inc(S["gn_pe"], 1)

            def spread(at, base, step):
                pe.wait_ge(S["gn_dve"], at("gn_dve", step))
                for c in range(CH):
                    mm = pe.matmul(maxb[:, 1, c:c + 1], indT[:, c * P:(c + 1) * P], gsum[:, base:base + 1],
                                   start=True, stop=True)
                mm.then_inc(S["gn_pe"], 1)

            def norm(at, stage):
                if stage == 0:
                    gather(at, lambda c: mv[:, c, 0:1], 2)
                elif stage == 1:
                    spread(at, 0, 3)
                elif stage == 2:
                    gather(at, lambda c: dev[:, c:c + 1], 7)
                elif stage == 3:
                    spread(at, 1, 8)

            for stage in range(4):
                norm(Unit(0, 0, 0, 0).at, stage)

            def unit(u):
                pe.wait_ge(S["xn_ready"], u.at("xn_ready", 1))
                pe.sem_inc(passed, 1)

                def q_freed(h, n):
                    pe.wait_ge(S[f"q_act{h}"], u.at(f"q_act{h}", n))
                    pe.wait_ge(S[f"q_dve{h}"], u.at(f"q_dve{h}", n))

                with pe.Fori(0, PAIRS // 2) as i:
                    for slot in range(2):
                        pe.wait_ge(S[f"wq_in{slot}"], u.at(f"wq_in{slot}", i * 16 + 16))
                        for h in range(2):
                            q_freed(h, i * 2 + slot)
                            for c in range(CH):
                                mm = pe.matmul(pjb[:, h, :], wq[:, slot, c, :], xn[:, c, h * HALF:(h + 1) * HALF],
                                               start=(c == 0), stop=(c == CH - 1))
                            mm.then_inc(S["q_ps"], 1)

                for h in range(2):
                    q_freed(h, PAIRS)
                pe.sem_inc(passed, 1)

                def k_products(n, first, end):
                    if first == 0:
                        pe.wait_ge(S["wk_in"], u.at("wk_in", n * 16 + 16))
                    for i in range(first, end):
                        h, c = divmod(i, CH)
                        mm = pe.matmul(pjb[:, h, :], wk[:, c, :], xn[:, c, h * HALF:(h + 1) * HALF],
                                       start=(c == 0), stop=(c == CH - 1))
                        if c == CH - 1:
                            mm.then_inc(S["k_ps"], 1)

                def v_tile(n, t, bank):
                    if t == 0:
                        pe.wait_ge(S["wv_in"], u.at("wv_in", n * 16 + 16))
                    for c in range(CH):
                        mm = pe.matmul(bank[:, t // 4, t % 4 * P:(t % 4 + 1) * P], xn[:, c, t * P:(t + 1) * P],
                                       wv[:, c, :], start=(c == 0), stop=(c == CH - 1))
                    if t % 4 == 3:
                        mm.then_inc(S["v_ps"], 1)

                def k_is_read(n):
                    pe.wait_ge(S["k_act"], u.at("k_act", n * 2 + 2))
                    pe.wait_ge(S["k_dve"], u.at("k_dve", n * 2 + 2))

                k_products(0, 0, 2 * CH)
                if u.kind == 0:
                    for t in range(QT):
                        v_tile(0, t, scb)
                    k_is_read(0)
                    k_products(1, 0, 2 * CH)
                    pe.wait_ge(S["v_done"], u.at("v_done", 2))
                    for t in range(QT):
                        v_tile(1, t, scb)
                    pe.wait_ge(S["v_done"], u.at("v_done", 4))
                    k_is_read(1)
                if u.kind:
                    rows = qo[:].rearrange("p n (h w) -> p n h w", w=SIDE)
                    for g in range(SIDE // 2):
                        slot = g // 2 % 2
                        if g % 2 == 0:
                            pe.wait_ge(S[f"wq_in{slot}"], u.at(f"wq_in{slot}", 16 * (3 + g // 4 + 1)))
                        if g >= 2:
                            pe.wait_ge(S["relh_done"], u.at("relh_done", g - 1))
                        for i in range(2):
                            r = 2 * g + i
                            mm = pe.matmul(scb[0:D, g % 2, i * 192:(i + 1) * 192],
                                           rel_tables(slot)[:, 0, r % RPL, :], rows[:, :, r, :],
                                           start=True, stop=True)
                        mm.then_inc(S["relh_ps"], 1)
                        if g >= 2:
                            pe.wait_ge(S["relw_done"], u.at("relw_done", g - 1))
                        for i in range(2):
                            r = 2 * g + i
                            mm = pe.matmul(maxb[D:P, g % 2, i * 192:(i + 1) * 192],
                                           rel_tables(slot)[:, 1, r % RPL, :], rows[:, :, :, r],
                                           start=True, stop=True)
                        mm.then_inc(S["relw_ps"], 1)
                    pe.wait_ge(S["relh_done"], u.at("relh_done", 16))
                    pe.wait_ge(S["relw_done"], u.at("relw_done", 16))
                    pe.sem_inc(passed, 1)

                def max_tile(head, par, e, t):
                    if t == 0:
                        pe.wait_ge(S["qr_ready"], u.at("qr_ready", head + 1))
                    if u.kind == 0:
                        if t >= 2:
                            pe.wait_ge(S["max_done"], u.at("max_done", head * QT + (t - 1)))
                        lo, hi = near(t)
                        mm = pe.matmul(maxb[:, t % 2, 0:(hi - lo) * P], qr[:, t * P:(t + 1) * P],
                                       kr[:, par, e, lo * P:hi * P], start=True, stop=True)
                    else:
                        if t >= 1:
                            pe.wait_ge(S["max_done"], u.at("max_done", head * QT + t))
                        for h in range(2):
                            mm = pe.matmul(maxb[:, h, :], qr[:, t * P:(t + 1) * P],
                                           kr[:, par, e, h * HALF:(h + 1) * HALF], start=True, stop=True)
                    mm.then_inc(S["max_ps"], 1)

                def shift(head):
                    for h in range(2):
                        pe.wait_ge(S["diag_ready"], u.at("diag_ready", head * 2 + h + 1))
                        if h == 0:
                            pe.wait_ge(S["max_done"], u.at("max_done", head * QT + QT))
                        pe.matmul(maxb[:, h, :], ones_r[:], diag[:, h, :], start=True, stop=True) \
                            .then_inc(S["shift_ps"], 1)

                def values(head, par, e, n):
                    done = head * STEPS[u.kind] + n + 1
                    kt, lo, _ = steps(u.kind)[n]
                    for part, buf in (("high_done", high), ("low_done", low)):
                        pe.wait_ge(S[part], u.at(part, done))
                        if n == 0 and buf is high:
                            pe.wait_ge(S["o_act"], u.at("o_act", head))
                            pe.wait_ge(S["o_dve"], u.at("o_dve", head))
                        for a, b, first in value_parts(u.kind, n):
                            mm = pe.matmul(pvb[:, a // HALF, a % HALF:(b - 1) % HALF + 1],
                                           vop[:, par, kt, e].rearrange("p a d -> p (a d)"),
                                           buf[:, n % NR, a - lo:b - lo], start=first and buf is high, stop=True,
                                           skip_group_check=True)
                    mm.then_inc(S["value_ps"], 1)

                def row_sums(head):
                    pe.wait_ge(S["tallied"], u.at("tallied", (head + 1) * TALLIES[u.kind]))
                    pe.wait_ge(S["sum_act"], u.at("sum_act", head))
                    for h in range(2):
                        mm = pe.matmul(pjb[:, h, :], ones[:], tally[:, h * HALF:(h + 1) * HALF],
                                       start=True, stop=True)
                    mm.then_inc(S["sum_ps"], 1)

                def window(head, n, par, e, after):
                    at = PLACES[u.kind]
                    more = after or e == 0
                    pe.wait_ge(S["shifted"], u.at("shifted", head + 1))
                    pe.wait_ge(S["qf_act"], u.at("qf_act", head + 1))
                    for s, (kt, lo, hi) in enumerate(steps(u.kind)):
                        if s >= 2:
                            pe.wait_ge(S["high_done"], u.at("high_done", head * STEPS[u.kind] + (s - 1)))
                        pe.matmul(scb[:, s % 2, 0:hi - lo], kop[:, par, e, kt * P:(kt + 1) * P],
                                  qf[:, e, lo:hi], start=True, stop=True).then_inc(S["score_ps"], 1)
                        if s >= 2:
                            values(head, par, e, s - 2)
                        if more:
                            for t, place in enumerate(at.maxima):
                                if place == s:
                                    max_tile(head + 1, (1 - par) if e else par, 1 - e, t)
                            if s == at.shift:
                                shift(head + 1)
                        if after and e == 0 and s in at.k:
                            i = at.k.index(s)
                            if i == 0:
                                pe.wait_ge(S["sum_act"], u.at("sum_act", head))
                            k_products(n + 1, 2 * i, 2 * i + 2)
                        if after and e == 1 and s in at.v:
                            i = at.v.index(s)
                            if i == 0:
                                pe.wait_ge(S["sum_act"], u.at("sum_act", head))
                            v_tile(n + 1, i, pjb)
                    values(head, par, e, STEPS[u.kind] - 2)
                    values(head, par, e, STEPS[u.kind] - 1)
                    if u.kind and after:
                        if e == 0:
                            k_is_read(n + 1)
                        else:
                            pe.wait_ge(S["v_done"], u.at("v_done", (n + 1) * 2 + 2))
                    row_sums(head)

                def pair(n, par, before, after):
                    window(n * 2, n, par, 0, after)
                    window(n * 2 + 1, n, par, 1, after)

                if u.kind:
                    k_is_read(0)
                for t in range(QT):
                    max_tile(0, 0, 0, t)
                    if u.kind:
                        v_tile(0, t, scb)
                shift(0)
                if u.kind:
                    pe.wait_ge(S["v_done"], u.at("v_done", 2))
                pairs_of(pe, pair)

                pe.wait_ge(S["sum_act"], u.at("sum_act", HEADS))
                of_q = RAISED["wq_in0"][u.kind] // 16 - 3

                def part(c, h, first, end):
                    bank = (pjb, scb)[c % 2]
                    for i in range(first, end):
                        mm = pe.matmul(bank[:, h, :], wq[:, c % 2, i, :], qo[:, i, h * HALF:(h + 1) * HALF],
                                       start=(i == 0), stop=(i == CH - 1))
                    if end == CH:
                        mm.then_inc(S["proj_ps"], 1)

                for c in range(CH):
                    pe.wait_ge(S[f"wq_in{c % 2}"], u.at(f"wq_in{c % 2}", 16 * (of_q + c // 2 + 1)))
                    if c == 0:
                        pe.wait_ge(S["norm_done"], u.at("norm_done", PARTS * (PAIRS - 1)))
                        for h in range(2):
                            part(c, h, 0, CH - 1)
                        pe.wait_ge(S["norm_done"], u.at("norm_done", PARTS * PAIRS))
                        for h in range(2):
                            part(c, h, CH - 1, CH)
                    for h in range(2):
                        if c >= 2:
                            pe.wait_ge(S[f"added{h}"], u.at(f"added{h}", c - 1))
                        if c >= 1:
                            part(c, h, 0, CH)
                        if 2 * c + h in GN_BESIDE:
                            norm(of_next(u), GN_BESIDE.index(2 * c + h))
                for h in range(2):
                    pe.wait_ge(S[f"added{h}"], u.at(f"added{h}", CH))

            units(pe, unit)

        @block.scalar
        def _(act):
            for name in LIFTED["act"]:
                act.sem_inc(S[name], START[name])
            for c in range(CH):
                act.dma_start(out[c * P:(c + 1) * P, :], xT_in[c * P:(c + 1) * P, :]).then_inc(copied, 16)

            def norm_root(at):
                act.wait_ge(S["gn_dve"], at("gn_dve", 9))
                act.activation(root[:], var[:], ACT.Sqrt).then_inc(S["gn_act"], 1)

            norm_root(Unit(0, 0, 0, 0).at)

            def unit(u):
                act.wait_ge(S["params_in"], u.at("params_in", RAISED["params_in"][u.kind]))
                with act.Fori(0, PAIRS) as p:
                    for h in range(2):
                        act.wait_ge(S["q_ps"], u.at("q_ps", p * 2 + h + 1))
                        act.sem_inc(passed, 1)
                        src, cols = pjb[0:D, h, :], slice(h * HALF, (h + 1) * HALF)
                        act.activation(qo[0:D, p, cols], src, ACT.Identity,
                                       bias=par[0:D, 0, bass.ds(p, 1)]).then_inc(S[f"q_act{h}"], 1)
                act.wait_ge(S["bk_ready"], u.at("bk_ready", 1))
                def k_read(n, par, h):
                    act.wait_ge(S["k_ps"], u.at("k_ps", n * 2 + h + 1))
                    act.sem_inc(passed, 1)
                    src, cols = pjb[0:D, h, :], slice(h * HALF, (h + 1) * HALF)
                    act.activation(kr[0:D, par, 0, cols], src, ACT.Identity, bias=bk8[0:D, bass.ds(n, 1)], scale=0.125)
                    act.activation(kop[0:D, par, 0, cols], src, ACT.Identity, bias=bk8[0:D, bass.ds(n, 1)],
                                   scale=0.125).then_inc(S["k_act"], 1)

                for n in range(2 if u.kind == 0 else 1):
                    for h in range(2):
                        k_read(n, n, h)
                if u.kind:
                    rows = relp[:].rearrange("r p (h w) -> r p h w", w=SIDE)
                    for g in range(SIDE // 2):
                        act.wait_ge(S["relh_ps"], u.at("relh_ps", g + 1))
                        for e in range(2):
                            src = scb[e * SIDE:(e + 1) * SIDE, g % 2, 0:2 * 192].rearrange(
                                "k (i p w) -> k i p w", i=2, w=SIDE)
                            dst = rows[e * D:e * D + SIDE, :, 2 * g:2 * g + 2, :].rearrange("k p i w -> k i p w")
                            a = act.activation(dst, src, ACT.Copy)
                        a.then_inc(S["relh_done"], 1)

                def query_operand(e, p):
                    act.sem_inc(passed, 1)
                    act.activation(qf[0:D, e, :], qo[e * D:(e + 1) * D, p, :], ACT.Copy)
                    act.activation(qf[D + SIDE:P, e, :], relp[e * D + SIDE:(e + 1) * D, p, :],
                                   ACT.Copy).then_inc(S["qf_act"], 1)

                for h in range(2):
                    act.wait_ge(S[f"q_dve{h}"], u.at(f"q_dve{h}", PAIRS))
                if u.kind:
                    act.wait_ge(S["relw_done"], u.at("relw_done", 16))
                else:
                    act.wait_ge(S["mask_in"], u.at("mask_in", 32))
                query_operand(0, 0)

                def window(head, n, par, e, after):
                    at = PLACES[u.kind]
                    for s, (kt, lo, hi) in enumerate(steps(u.kind)):
                        done = head * STEPS[u.kind] + s
                        act.wait_ge(S["score_ps"], u.at("score_ps", done + 1))
                        if s == 0:
                            act.wait_ge(S["sum_ps"], u.at("sum_ps", head))
                        if s >= NP + 2 * u.kind:
                            act.wait_ge(S["low_done"], u.at("low_done", done - (NP - 1)))
                            act.wait_ge(S["tallied"], u.at("tallied", head * TALLIES[u.kind]
                                                           + (s - (NP - 1) - 2 * u.kind)))
                        act.activation(raw(u.kind, s), scb[:, s % 2, 0:hi - lo], ACT.Exp) \
                            .then_inc(S["exp_done"], 1)
                        if s >= NR:
                            act.wait_ge(S["value_ps"], u.at("value_ps", done - (NR - 1)))
                        act.activation(high[:, s % NR, 0:hi - lo], scb[:, s % 2, 0:hi - lo],
                                       ACT.Exp).then_inc(S["high_done"], 1)
                        if s == at.qf and (after or e == 0):
                            query_operand(1 - e, n + e)
                        if after and e == 0 and s in at.k_read:
                            k_read(n + 1, 1 - par, at.k_read.index(s))
                    act.wait_ge(S["value_ps"], u.at("value_ps", (head + 1) * STEPS[u.kind]))
                    act.sem_inc(passed, 1)
                    act.activation(qo[e * D:(e + 1) * D, n, :].rearrange("p (a b) -> p a b", a=2),
                                   pvb[0:D, :, :], ACT.Copy).then_inc(S["o_act"], 1)
                    act.wait_ge(S["sum_ps"], u.at("sum_ps", head + 1))
                    act.sem_inc(passed, 1)
                    act.activation(relp[e * D:(e + 1) * D, n, :].rearrange("p (a b) -> p a b", a=2),
                                   pjb[e * D:(e + 1) * D, :, :], ACT.Copy).then_inc(S["sum_act"], 1)

                def pair(n, par, before, after):
                    window(n * 2, n, par, 0, after)
                    window(n * 2 + 1, n, par, 1, after)

                pairs_of(act, pair)

                for c in range(CH):
                    if c == ROOT_AT:
                        norm_root(of_next(u))
                    for h in range(2):
                        act.wait_ge(S[f"added{h}"], u.at(f"added{h}", c + 1))
                    act.dma_start(out[c * P:(c + 1) * P, bass.ds(u.image * TOK, TOK)], xe[:, c % 2, :]) \
                        .then_inc(S[f"stored{c % 2}"], 16)

            units(act, unit)

        @block.vector
        def _(dve):
            for name in LIFTED["dve"]:
                dve.sem_inc(S[name], START[name])
            dve.memset(ones[:], 1.0).then_inc(const_done, 1)
            dve.wait_ge(const_in, 16 * 7)
            dve.tensor_copy(kr[D:P, :, :, :], kop[D:P, :, :, :]).then_inc(const_done, 1)
            dve.wait_ge(const_done, 2)
            dve.tensor_copy(ones_r[:], ones[:]).then_inc(const_done, 1)
            dve.wait_ge(const_done, 3)

            def norm(at, stage):
                def did(ins, step):
                    ins.then_inc(S["gn_dve"], 1)
                    dve.wait_ge(S["gn_dve"], at("gn_dve", step))
                    dve.sem_inc(passed, 1)

                if stage in (0, 1):
                    if stage == 0:
                        dve.wait_ge(S["x_in"], at("x_in", 16 * CH))
                    for c in range(stage * CH // 2, (stage + 1) * CH // 2):
                        for h in range(2):
                            a = dve.bn_stats(bst[:, c, h, :], xn[:, c, h * HALF:(h + 1) * HALF])
                    if stage == 1:
                        did(a, 1)
                        for c in range(CH):
                            a = dve.bn_aggr(mv[:, c, :], bst[:, c].rearrange("p a b -> p (a b)"))
                        did(a, 2)
                elif stage == 2:
                    dve.wait_ge(S["gn_pe"], at("gn_pe", 1))
                    did(dve.tensor_scalar(gsum[:, 0:1], maxb[0:GROUPS, 0, 0:1], 1.0 / PER_GROUP, None, ALU.mult), 3)
                elif stage == 3:
                    dve.wait_ge(S["gn_pe"], at("gn_pe", 2))
                    dve.sem_inc(passed, 1)
                    did(dve.tensor_copy(cmean[:], maxb[:, 1, 0:CH]), 4)
                    did(dve.tensor_tensor(dev[:], mv[:, :, 0], cmean[:], ALU.subtract), 5)
                    did(dve.tensor_tensor(dev[:], dev[:], dev[:], ALU.mult), 6)
                    did(dve.tensor_tensor(dev[:], dev[:], mv[:, :, 1], ALU.add), 7)
                elif stage == 4:
                    dve.wait_ge(S["gn_pe"], at("gn_pe", 3))
                    did(dve.tensor_scalar(gsum[:, 1:2], maxb[0:GROUPS, 0, 0:1], 1.0 / PER_GROUP, None, ALU.mult), 8)
                elif stage == 5:
                    dve.wait_ge(S["gn_pe"], at("gn_pe", 4))
                    did(dve.tensor_scalar(var[:], maxb[:, 1, 0:CH], GN_EPS, None, ALU.add), 9)
                else:
                    dve.wait_ge(S["gn_act"], at("gn_act", 1))
                    dve.sem_inc(passed, 1)
                    did(dve.reciprocal(rstd[:], root[:]), 10)
                    did(dve.tensor_tensor(newt[:], rstd[:], rstd[:], ALU.mult), 11)
                    did(dve.tensor_tensor(newt[:], newt[:], var[:], ALU.mult), 12)
                    did(dve.tensor_scalar(newt[:], newt[:], -0.5, 1.5, ALU.mult, ALU.add), 13)
                    did(dve.tensor_tensor(rstd[:], rstd[:], newt[:], ALU.mult), 14)
                    did(dve.scalar_tensor_tensor(nshift[:], cmean[:], -1.0, rstd[:], ALU.mult, ALU.mult), 15)
                    for c in range(CH):
                        a = dve.tensor_scalar(xn[:, c, :], xn[:, c, :], rstd[:, c:c + 1],
                                              nshift[:, c:c + 1], ALU.mult, ALU.add)
                    a.then_inc(S["xn_ready"], 1)

            for stage in range(7):
                norm(Unit(0, 0, 0, 0).at, stage)

            def unit(u):
                dve.wait_ge(S["params_in"], u.at("params_in", RAISED["params_in"][u.kind]))
                dve.tensor_scalar(bk8[:], par[:, 1, :], 0.125, None, ALU.mult).then_inc(S["bk_ready"], 1)
                with dve.Fori(0, PAIRS) as p:
                    for h in range(2):
                        dve.wait_ge(S["q_ps"], u.at("q_ps", p * 2 + h + 1))
                        src, cols = pjb[D:P, h, :], slice(h * HALF, (h + 1) * HALF)
                        dve.tensor_scalar(qo[D:P, p, cols], src, par[D:P, 0, bass.ds(p, 1)], None,
                                          ALU.add).then_inc(S[f"q_dve{h}"], 1)
                def k_read(n, par, h):
                    dve.wait_ge(S["k_ps"], u.at("k_ps", n * 2 + h + 1))
                    src, cols = pjb[D:P, h, :], slice(h * HALF, (h + 1) * HALF)
                    dve.tensor_scalar(kr[0:D, par, 1, cols], src, 0.125, bk8[D:P, bass.ds(n, 1)], ALU.mult, ALU.add)
                    dve.tensor_scalar(kop[0:D, par, 1, cols], src, 0.125, bk8[D:P, bass.ds(n, 1)], ALU.mult,
                                      ALU.add).then_inc(S["k_dve"], 1)

                def v_read(n, par, g, bank):
                    dve.wait_ge(S["v_done"], u.at("v_done", n * 2 + g))
                    dve.wait_ge(S["v_ps"], u.at("v_ps", n * 2 + g + 1))
                    bias = bv[:, bass.ds(n * P, P)].rearrange("p (e d) -> p e d", e=2).unsqueeze(1)
                    dve.tensor_tensor(vraw[:], bank[:, g, :].rearrange("p (t e d) -> p t e d", t=4, e=2),
                                      bias.to_broadcast([P, 4, 2, D]), ALU.add).then_inc(S["v_step"], 1)
                    dve.wait_ge(S["v_step"], u.at("v_step", n * 4 + 2 * g + 1))
                    dve.sem_inc(passed, 1)
                    rounded, rest = (vop[:, par, 4 * g:4 * g + 4, :, part, :] for part in range(2))
                    dve.tensor_copy(rounded, vraw[:]).then_inc(S["v_step"], 1)
                    dve.wait_ge(S["v_step"], u.at("v_step", n * 4 + 2 * g + 2))
                    dve.tensor_tensor(rest, vraw[:], rounded.bitcast(F32), ALU.subtract).then_inc(S["v_done"], 1)

                dve.wait_ge(S["bk_ready"], u.at("bk_ready", 1))
                for n in range(2 if u.kind == 0 else 1):
                    for h in range(2):
                        k_read(n, n, h)
                    if u.kind == 0:
                        v_read(n, n, 0, scb)
                        v_read(n, n, 1, scb)
                if u.kind:
                    rows = relp[:].rearrange("r p (h w) -> r p h w", w=SIDE)
                    for g in range(SIDE // 2):
                        dve.wait_ge(S["relw_ps"], u.at("relw_ps", g + 1))
                        for e in range(2):
                            src = maxb[D + e * SIDE:D + (e + 1) * SIDE, g % 2, 0:2 * 192].rearrange(
                                "k (i p h) -> k i p h", i=2, h=SIDE)
                            dst = rows[e * D + SIDE:(e + 1) * D, :, :, 2 * g:2 * g + 2].rearrange("k p h i -> k i p h")
                            a = dve.tensor_copy(dst, src)
                        a.then_inc(S["relw_done"], 1)

                def round_q(head, e, p):
                    dve.tensor_copy(qr[0:D, :], qo[e * D:(e + 1) * D, p, :])
                    dve.tensor_copy(qr[D:P, :], relp[e * D:(e + 1) * D, p, :]).then_inc(S["qr_ready"], 1)

                def reduce(head, e, t):
                    dve.wait_ge(S["max_ps"], u.at("max_ps", head * QT + t + 1))
                    if u.kind == 0:
                        src = maxb[:, t % 2, 0:(near(t)[1] - near(t)[0]) * P]
                    else:
                        src = maxb[:].rearrange("p a b -> p (a b)")
                    dve.tensor_reduce(negmax[:, e, t:t + 1], src, AX.X, ALU.max, negate=True) \
                        .then_inc(S["max_done"], 1)

                def shift(head, e, p):
                    dve.wait_ge(S["shift_ps"], u.at("shift_ps", head * 2 + 2))
                    rows, terms = (x.rearrange("p (a b) -> p a b", a=2)
                                   for x in (qf[D:D + SIDE, e, :], relp[e * D:e * D + SIDE, p, :]))
                    dve.tensor_tensor(rows, maxb[D:D + SIDE, :, :], terms, ALU.add).then_inc(S["shifted"], 1)

                def split(head, s):
                    done = head * STEPS[u.kind] + s
                    _, lo, hi = steps(u.kind)[s]
                    dve.wait_ge(S["high_done"], u.at("high_done", done + 1))
                    if s >= NR:
                        dve.wait_ge(S["value_ps"], u.at("value_ps", done - (NR - 1)))
                    dve.tensor_tensor(low[:, s % NR, 0:hi - lo], raw(u.kind, s),
                                      high[:, s % NR, 0:hi - lo].bitcast(F32), ALU.subtract) \
                        .then_inc(S["low_done"], 1)

                def add_low(head, e, p):
                    dve.wait_ge(S["o_act"], u.at("o_act", head + 1))
                    o = qo[e * D:(e + 1) * D, p, :].rearrange("p (a b) -> p a b", a=2)
                    dve.tensor_tensor(o, pvb[D:P, :, :], o, ALU.add).then_inc(S["o_dve"], 1)

                def divide(n, part):
                    if part == 0:
                        dve.wait_ge(S["o_dve"], u.at("o_dve", n * 2 + 2))
                        dve.wait_ge(S["sum_act"], u.at("sum_act", n * 2 + 2))
                        dve.sem_inc(passed, 1)
                    cols = slice(part * (TOK // PARTS), (part + 1) * (TOK // PARTS))
                    dve.reciprocal(relp[:, n, cols], relp[:, n, cols]).then_inc(S["recip_done"], 1)
                    dve.wait_ge(S["recip_done"], u.at("recip_done", n * PARTS + part + 1))
                    dve.tensor_tensor(qo[:, n, cols], qo[:, n, cols], relp[:, n, cols], ALU.mult) \
                        .then_inc(S["norm_done"], 1)

                def window(head, n, par, e, before, after):
                    at = PLACES[u.kind]
                    more = after or e == 0
                    for s in range(STEPS[u.kind]):
                        split(head, s)
                        if more:
                            for t, place in enumerate(at.maxima):
                                if place == s:
                                    reduce(head + 1, 1 - e, t)
                            if s == at.shift:
                                shift(head + 1, 1 - e, n + e)
                        if after and s == at.round_q:
                            round_q(head + 2, e, n + 1)
                        if before and s in at.divide[e]:
                            divide(n - 1, at.divide[e].index(s) + e * PARTS // 2)
                        if after and e == 0 and s in at.k_read:
                            k_read(n + 1, 1 - par, at.k_read.index(s))
                        if after and e == 1 and s in at.v_read:
                            v_read(n + 1, 1 - par, at.v_read.index(s), pjb)
                    add_low(head, e, n)

                def pair(n, par, before, after):
                    window(n * 2, n, par, 0, before, after)
                    window(n * 2 + 1, n, par, 1, before, after)

                for h in range(2):
                    dve.wait_ge(S[f"q_act{h}"], u.at(f"q_act{h}", PAIRS))
                    dve.wait_ge(S[f"q_dve{h}"], u.at(f"q_dve{h}", PAIRS))
                if u.kind:
                    dve.wait_ge(S["relh_done"], u.at("relh_done", 16))
                    dve.wait_ge(S["relw_done"], u.at("relw_done", 16))
                else:
                    dve.wait_ge(S["mask_in"], u.at("mask_in", 32))
                dve.sem_inc(passed, 1)
                round_q(0, 0, 0)
                for t in range(QT):
                    reduce(0, 0, t)
                    if u.kind and t == 4:
                        v_read(0, 0, 0, scb)
                round_q(1, 1, 0)
                shift(0, 0, 0)
                if u.kind:
                    v_read(0, 0, 1, scb)
                pairs_of(dve, pair)
                for part in range(PARTS):
                    divide(PAIRS - 1, part)

                for c in range(CH):
                    dve.wait_ge(S[f"xe_in{c % 2}"], u.at(f"xe_in{c % 2}", 16 * (c // 2 + 1)))
                    for h in range(2):
                        dve.wait_ge(S["proj_ps"], u.at("proj_ps", c * 2 + h + 1))
                        cols = slice(h * HALF, (h + 1) * HALF)
                        dve.scalar_tensor_tensor(xe[:, c % 2, cols], (pjb, scb)[c % 2][:, h, :], par[:, 2, c:c + 1],
                                                 xe[:, c % 2, cols], ALU.add, ALU.add).then_inc(S[f"added{h}"], 1)
                        j = 2 * c + h
                        if j in GN_AFTER:
                            norm(of_next(u), GN_AFTER.index(j))

            units(dve, unit)

        @block.gpsimd
        def _(pool):
            pool.wait_ge(const_in, 16 * 7)

            def unit(u):
                def diagonals(head, e, h):
                    pool.wait_ge(S["max_done"], u.at("max_done", head * QT + 4 * h + 4))
                    pool.wait_ge(S["shift_ps"], u.at("shift_ps", head * 2))
                    pool.tensor_tensor(
                        diag[:, h, :].rearrange("p (t q) -> p t q", t=4),
                        ident[:].unsqueeze(1).to_broadcast([P, 4, P]),
                        negmax[:, e, 4 * h:4 * h + 4].unsqueeze(2).to_broadcast([P, 4, P]),
                        ALU.mult).then_inc(S["diag_ready"], 1)

                def add_up(head, s):
                    done = head * STEPS[u.kind] + s
                    kt, lo, hi = steps(u.kind)[s]
                    if u.kind and s < 2:
                        return
                    pool.wait_ge(S["exp_done"], u.at("exp_done", done + 1))
                    if u.kind and s < 4:
                        pool.wait_ge(S["low_done"], u.at("low_done", done - 1))
                    if s > 2 * u.kind:
                        pool.wait_ge(S["tallied"], u.at("tallied", head * TALLIES[u.kind] + (s - 2 * u.kind)))
                    known = hi if u.kind else max(near(kt - 1)[1] * P if kt else 0, lo)
                    src = probs[:, s % NP, :]
                    if known < hi:
                        pool.sem_inc(passed, 1)
                        a = pool.tensor_copy(tally[:, known:hi], src[:, known - lo:hi - lo])
                    if known > lo:
                        a = pool.tensor_tensor(tally[:, lo:known], tally[:, lo:known], src[:, 0:known - lo], ALU.add)
                    a.then_inc(S["tallied"], 1)

                def window(head, e, more):
                    for s in range(STEPS[u.kind]):
                        add_up(head, s)
                        if more and s in PLACES[u.kind].diag:
                            diagonals(head + 1, 1 - e, PLACES[u.kind].diag.index(s))

                def pair(n, par, before, after):
                    window(n * 2, 0, True)
                    window(n * 2 + 1, 1, after)

                for h in range(2):
                    diagonals(0, 0, h)
                pairs_of(pool, pair)

            units(pool, unit)


_SHAPES = [("xT_in", (C, IMAGES * TOK)), ("wq_in", (LAYERS, PAIRS, P, CH, P)), ("wk_in", (LAYERS, PAIRS, P, CH, P)),
           ("wv_in", (LAYERS, PAIRS, P, CH, P)), ("wo_in", (LAYERS, PAIRS, P, CH, P)),
           ("params_in", (LAYERS, P, 3, CH)), ("bv_in", (LAYERS, C)), ("rel_in", (LAYERS - 1, SIDE // RPL, P, 2, RPL, D)),
           ("onehot_in", (2 * SIDE, TOK)), ("mask_in", (2 * SIDE, TOK)), ("ident_in", (P, P)),
           ("ind_in", (P, CH, GROUPS)), ("indT_in", (GROUPS, C))]


def lay_out(inputs):
    import numpy as np

    def blocks(w):
        n = w.shape[1] // P
        full = np.zeros((PAIRS, P, CH, P), np.float32)
        full[:n] = w.reshape(CH, P, n, P).transpose(2, 1, 0, 3)
        return full

    g = {k: np.asarray(v) for k, v in inputs.items()}
    kv0 = KV_PAIRS0 * P
    wT = [g["L0_conv_w_qkv"].T, g["L1_conv_qkv_w"].T, g["L2_conv_qkv_w"].T, g["L3_conv_w_qkv"]]
    cuts = [(C, C + kv0)] + [(C, 2 * C)] * 3
    zero = np.zeros((C,), np.float32)
    qkvb = [None, g["L1_conv_qkv_b"], g["L2_conv_qkv_b"], g["L3_conv_b_qkv"]]
    ob = [zero, g["L1_conv_proj_b"], g["L2_conv_proj_b"], g["L3_conv_b_proj"]]
    wo = [g["L0_conv_w_out"].T, g["L1_conv_proj_w"].T, g["L2_conv_proj_w"].T, g["L3_conv_w_proj"]]

    def bias(i, part):
        return zero if qkvb[i] is None else qkvb[i][part * C:(part + 1) * C]

    params = np.stack([np.stack([b.reshape(CH, P).T for b in (bias(i, 0), bias(i, 1), ob[i])], axis=1)
                       for i in range(LAYERS)])
    rel = np.zeros((LAYERS - 1, P, 2, SIDE, 2, SIDE), np.float32)
    which = np.arange(SIDE)[:, None] - np.arange(SIDE)[None] + SIDE - 1
    for i, layer in ((0, "L1"), (2, "L3")):
        for a, axis in enumerate(("h", "w")):
            table = g[f"{layer}_conv_rel_pos_{axis}"][which].transpose(2, 0, 1)
            rel[i, 0:D, a, :, 0] = table
            rel[i, D:P, a, :, 1] = table
    rel = rel.reshape(LAYERS - 1, P, 2, SIDE // RPL, RPL, D).transpose(0, 3, 1, 2, 4, 5)
    row, col = np.divmod(np.arange(TOK), SIDE)
    k = np.arange(SIDE)[:, None]

    def window(at):
        first = np.clip(at - KSIZE // 2, 0, SIDE - KSIZE)[None]
        return np.where((k >= first) & (k < first + KSIZE), 0.0, MASKED)

    group = np.arange(C) // PER_GROUP
    ind = (group[:, None] == np.arange(GROUPS)).astype(np.float32)
    return {
        "xT_in": g["x"].reshape(IMAGES * TOK, C).T,
        "wq_in": np.stack([blocks(w[:, :C]) for w in wT]),
        "wk_in": np.stack([blocks(w[:, a:b]) for w, (a, b) in zip(wT, cuts)]),
        "wv_in": np.stack([blocks(w[:, b:]) for w, (a, b) in zip(wT, cuts)]),
        "wo_in": np.stack([blocks(w) for w in wo]),
        "params_in": params,
        "bv_in": np.stack([bias(i, 2) for i in range(LAYERS)]),
        "rel_in": rel,
        "onehot_in": np.concatenate([k == row, k == col]).astype(np.float32),
        "mask_in": np.concatenate([window(row), window(col)]).astype(np.float32),
        "ident_in": np.eye(P, dtype=np.float32),
        "ind_in": ind.reshape(CH, P, GROUPS).transpose(1, 0, 2),
        "indT_in": ind.T,
    }


def kernel(**inputs):
    import numpy as np
    import concourse.bacc as bacc
    from concourse.bass_utils import run_bass_kernel_spmd

    nc = bacc.Bacc("TRN2", target_bir_lowering=False, num_devices=1)
    laid = lay_out(inputs)
    arrays, args = {}, {}
    for name, shape in _SHAPES:
        arrays[name] = np.ascontiguousarray(laid[name])
        assert arrays[name].shape == shape and arrays[name].dtype == np.float32, name
        args[name] = nc.dram_tensor(name, shape, F32, kind="ExternalInput").ap()
    out = nc.dram_tensor("out", (C, IMAGES * TOK), F32, kind="ExternalOutput").ap()
    build(nc, out=out, **args)
    r = run_bass_kernel_spmd(nc, [arrays], core_ids=[0])
    return np.ascontiguousarray(r.results[0]["out"].T).reshape(IMAGES, SIDE, SIDE, C)
```

```python
from contextlib import ExitStack

import concourse.bass as bass
from concourse import mybir

F32 = mybir.dt.float32
F32R = mybir.dt.float32r
ALU = mybir.AluOpType
ACT = mybir.ActivationFunctionType
AX = mybir.AxisListType

P = 128
SIDE = 32
TOK = SIDE * SIDE
IMAGES = 2
C = 768
CH = C // P
D = 64
PAIRS = C // (2 * D)
KV_PAIRS0 = 2
GROUPS = 32
PER_GROUP = C // GROUPS
HALF = 512
QT = TOK // P
REL = 2 * SIDE - 1
RPL = 4
KSIZE = 7
GN_EPS = 1e-5
MASKED = -float(2.0 ** 60)
LAYERS = 4


def near(t):
    return max(t - 1, 0), min(t + 1, QT - 1) + 1


def steps(kind):
    if kind == 0:
        return [(kt, near(kt)[0] * P, near(kt)[1] * P) for kt in range(QT)]
    return [(kt, q, q + HALF) for kt in range(QT) for q in (0, HALF)]


def value_parts(kind, n):
    kt, lo, hi = steps(kind)[n]
    cuts = [(a, b) for a, b in ((lo, min(hi, HALF)), (max(lo, HALF), hi)) if a < b]
    before = steps(kind)[:n]
    return [(a, b, not any(s[1] < (a // HALF + 1) * HALF and s[2] > a // HALF * HALF for s in before))
            for a, b in cuts]


class Places:

    def __init__(self, maxima, round_q, shift, qf, divide, k, k_read, v, v_read, diag):
        self.maxima = maxima
        self.round_q = round_q
        self.shift = shift
        self.qf = qf
        self.divide = divide
        self.k, self.k_read = k, k_read
        self.v, self.v_read = v, v_read
        self.diag = diag


PLACES = (
    Places(maxima=(1, 2, 2, 2, 3, 4, 5), round_q=(6, 7), shift=6, qf=(2, 5),
           divide=((1, 2, 5, 6), (1, 3, 5, 6)), k=(), k_read=(), v=(), v_read=(), diag=(2, 4)),
    Places(maxima=(2, 3, 5, 6, 7, 9, 10), round_q=(14, 14), shift=12, qf=(3, 4),
           divide=((5, 7, 9, 12), (1, 4, 10, 13)), k=(2, 4, 5, 6, 7, 9), k_read=(5, 7, 10, 12),
           v=(2, 3, 4, 5, 7, 8, 9, 11), v_read=(7, 10), diag=(5, 10)),
)
PARTS = 8

KV = (KV_PAIRS0, PAIRS)
STEPS = (len(steps(0)), len(steps(1)))
HEADS = 2 * PAIRS
GN_STEPS = 15
RAISED = {
    "params_in": (16 * 2, 16 * 2), "mask_in": (32, 0),
    "wq_in0": (16 * 6, 16 * 10), "wq_in1": (16 * 6, 16 * 10),
    "wk_in": (16 * KV[0], 16 * KV[1]), "wv_in": (16 * KV[0], 16 * KV[1]),
    "x_in": (16 * 6, 16 * 6), "xe_in0": (16 * 3, 16 * 3), "xe_in1": (16 * 3, 16 * 3),
    "stored0": (16 * 3, 16 * 3), "stored1": (16 * 3, 16 * 3),
    "gn_dve": (GN_STEPS, GN_STEPS), "gn_pe": (4, 4), "gn_act": (1, 1), "xn_ready": (1, 1),
    "q_ps": (12, 12), "q_act0": (6, 6), "q_act1": (6, 6), "q_dve0": (6, 6), "q_dve1": (6, 6), "bk_ready": (1, 1),
    "relh_ps": (0, 16), "relw_ps": (0, 16), "relh_done": (0, 16), "relw_done": (0, 16),
    "k_ps": (2 * KV[0], 2 * KV[1]), "k_act": (4 * KV[0], 4 * KV[1]), 
    "v_ps": (2 * KV[0], 2 * KV[1]), "v_done": (2 * KV[0], 2 * KV[1]),
    "qr_ready": (2 * HEADS, 2 * HEADS), "max_ps": (QT * HEADS, QT * HEADS), "max_done": (QT * HEADS, QT * HEADS),
    "diag_ready": (2 * HEADS, 2 * HEADS), "shift_ps": (2 * HEADS, 2 * HEADS), "shifted": (HEADS, HEADS),
    "score_ps": (HEADS * STEPS[0], HEADS * STEPS[1]), "exp_done": (HEADS * STEPS[0], HEADS * STEPS[1]),
    "value_ps": (HEADS * STEPS[0], HEADS * STEPS[1]), "o_act": (HEADS, HEADS), "o_dve": (HEADS, HEADS), "sum_act": (HEADS, HEADS),
    "qf_act": (HEADS, HEADS), "high_done": (HEADS * STEPS[0], HEADS * STEPS[1]),
    "low_done": (HEADS * STEPS[0], HEADS * STEPS[1]),
    "tallied": (HEADS * STEPS[0], HEADS * (STEPS[1] - 2)), "sum_ps": (HEADS, HEADS),
    "v_step": (4 * KV[0], 4 * KV[1]), "recip_done": (8 * PAIRS, 8 * PAIRS), "norm_done": (8 * PAIRS, 8 * PAIRS),
    "proj_ps": (12, 12), "added0": (6, 6), "added1": (6, 6),
}
LIFTED = {"pe": ("k_ps", "v_ps", "proj_ps", "shift_ps", "sum_ps", "max_ps", "value_ps"), "act": ("q_act0", "q_act1", "o_act", "sum_act", "stored0", "stored1",
                                               "high_done"),
          "pool": ("tallied",),
          "dve": ("q_dve0", "q_dve1", "v_done", "o_dve", "added0", "added1", "low_done")}
START = {name: 1 for names in LIFTED.values() for name in names}
START.update(proj_ps=3, sum_ps=2, value_ps=4, high_done=2, low_done=4, tallied=4)
NP = 4
NR = 4
GN_BESIDE = (4, 5, 6, 7)
ROOT_AT = 4
GN_AFTER = (0, 2, 4, 5, 6, 7, 8)
TALLIES = tuple(RAISED["tallied"][k] // HEADS for k in range(2))


class Unit:

    def __init__(self, kind, n, image, layer):
        self.kind, self.n, self.image, self.layer = kind, n, image, layer

    def at(self, name, local):
        first = START.get(name, 0) + (IMAGES * RAISED[name][0] if self.kind else 0)
        return self.n * RAISED[name][self.kind] + (local + first)


def build(nc, xT_in, wq_in, wk_in, wv_in, wo_in, params_in, bv_in, rel_in, onehot_in, mask_in,
          ident_in, ind_in, indT_in, out):
    with ExitStack() as ctx:
        def sb(name, shape, dt=F32):
            return ctx.enter_context(nc.sbuf_tensor(name, shape, dt))

        def ps(name):
            return ctx.enter_context(nc.psum_tensor(name, [P, 2, HALF], F32))

        xn = sb("xn", [P, CH, TOK])
        xe = sb("xe", [P, 2, TOK])
        relp = sb("relp", [P, PAIRS, TOK])
        qf = sb("qf", [P, 2, TOK])
        qo = sb("qo", [P, PAIRS, TOK])
        kop = sb("kop", [P, 2, 2, TOK])
        kr = sb("kr", [P, 2, 2, TOK], F32R)
        qr = sb("qr", [P, TOK], F32R)
        vop = sb("vop", [P, 2, QT, 2, 2, D], F32R)
        vraw = sb("vraw", [P, 4, 2, D])
        probs = sb("probs", [P, NP, HALF])
        high = sb("high", [P, NR, HALF], F32R)
        low = sb("low", [P, NR, HALF], F32R)
        tally = sb("tally", [P, 2, TOK])
        diag = sb("diag", [P, 2, HALF], F32R)
        wq = sb("wq", [P, 2, CH, P])
        wk = sb("wk", [P, CH, P])
        wv = sb("wv", [P, CH, P])
        par = sb("par", [P, 3, CH])
        bk8 = sb("bk8", [P, PAIRS])
        bv = sb("bv", [P, C])
        ident = sb("ident", [P, P])
        ones = sb("ones", [P, P])
        ones_r = sb("ones_r", [P, P], F32R)
        ind = sb("ind", [P, CH, GROUPS])
        indT = sb("indT", [GROUPS, C])
        negmax = sb("negmax", [P, 2, QT])
        bst = sb("bst", [P, CH, 2, 6])
        mv = sb("mv", [P, CH, 2])
        gsum = sb("gsum", [GROUPS, 2])
        cmean = sb("cmean", [P, CH])
        dev = sb("dev", [P, CH])
        var = sb("var", [P, CH])
        root = sb("root", [P, CH])
        rstd = sb("rstd", [P, CH])
        newt = sb("newt", [P, CH])
        nshift = sb("nshift", [P, CH])

        maxb, scb, pvb, pjb = ps("maxb"), ps("scb"), ps("pvb"), ps("pjb")

        S = {name: ctx.enter_context(nc.semaphore(name)) for name in RAISED}
        const_in = ctx.enter_context(nc.semaphore("const_in"))
        const_done = ctx.enter_context(nc.semaphore("const_done"))
        copied = ctx.enter_context(nc.semaphore("copied"))
        passed = ctx.enter_context(nc.semaphore("passed"))
        block = ctx.enter_context(nc.Block())

        def rel_tables(slot):
            flat = wq[:, slot].rearrange("p c o -> p (c o)")[:, 0:2 * RPL * D]
            return flat.rearrange("p (a r k) -> p a r k", a=2, r=RPL)

        def raw(kind, e, s):
            _, lo, hi = steps(kind)[s]
            return tally[:, e, lo:hi] if kind and s < 2 else probs[:, s % NP, 0:hi - lo]

        def units(eng, body):
            with eng.Fori(0, IMAGES) as b:
                body(Unit(0, b, b, 0))
            with eng.Fori(0, LAYERS - 1) as layer:
                with eng.Fori(0, IMAGES) as b:
                    body(Unit(1, layer * IMAGES + b, b, layer + 1))

        def pairs_of(eng, body):
            body(0, 0, False, True)
            with eng.Fori(0, (PAIRS - 2) // 2) as i:
                body(i * 2 + 1, 1, True, True)
                body(i * 2 + 2, 0, True, True)
            body(PAIRS - 1, 1, True, False)

        def of_next(u):
            return lambda name, local: u.at(name, local + RAISED[name][u.kind])

        @block.sync
        def _(sp):
            for c in range(CH):
                sp.dma_start(xn[:, c, :], xT_in[c * P:(c + 1) * P, 0:TOK]).then_inc(S["x_in"], 16)

            def unit(u):
                for slot in range(2):
                    sp.wait_ge(S["proj_ps"], u.at("proj_ps", 2 * slot - 2))
                    sp.dma_start(wq[:, slot], wq_in[u.layer, slot]).then_inc(S[f"wq_in{slot}"], 16)
                for h in range(2):
                    sp.wait_ge(S[f"added{h}"], u.at(f"added{h}", 0))
                sp.dma_start(par[:], params_in[u.layer]).then_inc(S["params_in"], 16)
                sp.dma_start(bv[:], bv_in[u.layer].partition_broadcast(P)).then_inc(S["params_in"], 16)
                if u.kind == 0:
                    for e in range(2):
                        for_all = mask_in.unsqueeze(1).to_broadcast([D, PAIRS, TOK])
                        sp.dma_start(relp[e * D:(e + 1) * D, :, :], for_all).then_inc(S["mask_in"], 16)
                with sp.Fori(1, PAIRS // 2) as i:
                    for slot in range(2):
                        sp.wait_ge(S["q_ps"], u.at("q_ps", i * 4 + (2 * slot - 2)))
                        sp.dma_start(wq[:, slot], wq_in[u.layer, i * 2 + slot]).then_inc(S[f"wq_in{slot}"], 16)

                def kv_weights(n):
                    sp.wait_ge(S["k_ps"], u.at("k_ps", n * 2))
                    sp.dma_start(wk[:], wk_in[u.layer, n]).then_inc(S["wk_in"], 16)
                    sp.wait_ge(S["v_ps"], u.at("v_ps", n * 2))
                    sp.dma_start(wv[:], wv_in[u.layer, n]).then_inc(S["wv_in"], 16)

                kv_weights(0)
                if u.kind:
                    for n in range(SIDE // RPL):
                        if n < 2:
                            sp.wait_ge(S["q_ps"], u.at("q_ps", 12))
                        else:
                            sp.wait_ge(S["relw_ps"], u.at("relw_ps", 2 * n - 2))
                        sp.dma_start(rel_tables(n % 2), rel_in[u.layer - 1, n]).then_inc(S[f"wq_in{n % 2}"], 16)
                with sp.Fori(1, KV[u.kind]) as n:
                    kv_weights(n)

                sp.wait_ge(S["k_ps"], u.at("k_ps", 2 * KV[u.kind]))
                sp.wait_ge(S["v_ps"], u.at("v_ps", 2 * KV[u.kind]))
                for h in range(2):
                    sp.wait_ge(S[f"stored{h}"], u.at(f"stored{h}", 0))
                sp.wait_ge(copied, 16 * CH)
                for c in range(CH):
                    sp.dma_start(xn[:, c, :], out[c * P:(c + 1) * P, bass.ds(u.image * -TOK + TOK, TOK)]) \
                        .then_inc(S["x_in"], 16)

                for c in range(CH):
                    slot = c % 2
                    if c < 2:
                        sp.wait_ge(*((S["relw_ps"], u.at("relw_ps", SIDE // 2)) if u.kind else
                                     (S["q_ps"], u.at("q_ps", 12))))
                    else:
                        sp.wait_ge(S["proj_ps"], u.at("proj_ps", 2 * c - 2))
                    sp.dma_start(wq[:, slot], wo_in[u.layer, c]).then_inc(S[f"wq_in{slot}"], 16)
                    sp.wait_ge(S[f"stored{slot}"], u.at(f"stored{slot}", 16 * (c // 2)))
                    sp.dma_start(xe[:, slot, :], out[c * P:(c + 1) * P, bass.ds(u.image * TOK, TOK)]) \
                        .then_inc(S[f"xe_in{slot}"], 16)

            units(sp, unit)
            for slot in range(2):
                sp.wait_ge(S[f"stored{slot}"], START[f"stored{slot}"] + 16 * 3 * LAYERS * IMAGES)
            sp.wait_ge(S["x_in"], 16 * 6 * (LAYERS * IMAGES + 1))

        @block.tensor
        def _(pe):
            for name in LIFTED["pe"]:
                pe.sem_inc(S[name], START[name])
            pe.wait_ge(const_in, 16 * 7)
            pe.wait_ge(const_done, 3)

            def gather(at, rhs, step):
                pe.wait_ge(S["gn_dve"], at("gn_dve", step))
                for c in range(CH):
                    mm = pe.matmul(maxb[0:GROUPS, 0, 0:1], ind[:, c, :], rhs(c), start=(c == 0), stop=(c == CH - 1))
                mm.then_inc(S["gn_pe"], 1)

            def spread(at, base, step):
                pe.wait_ge(S["gn_dve"], at("gn_dve", step))
                for c in range(CH):
                    mm = pe.matmul(maxb[:, 1, c:c + 1], indT[:, c * P:(c + 1) * P], gsum[:, base:base + 1],
                                   start=True, stop=True)
                mm.then_inc(S["gn_pe"], 1)

            def norm(at, stage):
                if stage == 0:
                    gather(at, lambda c: mv[:, c, 0:1], 2)
                elif stage == 1:
                    spread(at, 0, 3)
                elif stage == 2:
                    gather(at, lambda c: dev[:, c:c + 1], 7)
                elif stage == 3:
                    spread(at, 1, 8)

            for stage in range(4):
                norm(Unit(0, 0, 0, 0).at, stage)

            def unit(u):
                pe.wait_ge(S["xn_ready"], u.at("xn_ready", 1))
                pe.sem_inc(passed, 1)

                def q_freed(h, n):
                    pe.wait_ge(S[f"q_act{h}"], u.at(f"q_act{h}", n))
                    pe.wait_ge(S[f"q_dve{h}"], u.at(f"q_dve{h}", n))

                with pe.Fori(0, PAIRS // 2) as i:
                    for slot in range(2):
                        pe.wait_ge(S[f"wq_in{slot}"], u.at(f"wq_in{slot}", i * 16 + 16))
                        for h in range(2):
                            q_freed(h, i * 2 + slot)
                            for c in range(CH):
                                mm = pe.matmul(pjb[:, h, :], wq[:, slot, c, :], xn[:, c, h * HALF:(h + 1) * HALF],
                                               start=(c == 0), stop=(c == CH - 1))
                            mm.then_inc(S["q_ps"], 1)

                for h in range(2):
                    q_freed(h, PAIRS)
                pe.sem_inc(passed, 1)

                def k_products(n, first, end):
                    if first == 0:
                        pe.wait_ge(S["wk_in"], u.at("wk_in", n * 16 + 16))
                    for i in range(first, end):
                        h, c = divmod(i, CH)
                        mm = pe.matmul(pjb[:, h, :], wk[:, c, :], xn[:, c, h * HALF:(h + 1) * HALF],
                                       start=(c == 0), stop=(c == CH - 1))
                        if c == CH - 1:
                            mm.then_inc(S["k_ps"], 1)

                def v_tile(n, t, bank):
                    if t == 0:
                        pe.wait_ge(S["wv_in"], u.at("wv_in", n * 16 + 16))
                    for c in range(CH):
                        mm = pe.matmul(bank[:, t // 4, t % 4 * P:(t % 4 + 1) * P], xn[:, c, t * P:(t + 1) * P],
                                       wv[:, c, :], start=(c == 0), stop=(c == CH - 1))
                    if t % 4 == 3:
                        mm.then_inc(S["v_ps"], 1)

                def k_is_read(n):
                    pe.wait_ge(S["k_act"], u.at("k_act", n * 4 + 4))

                for h in range(2):
                    pe.wait_ge(S[f"added{h}"], u.at(f"added{h}", 0))
                if u.kind == 0:
                    k_products(0, 0, 2 * CH)
                    for t in range(QT):
                        v_tile(0, t, scb)
                    k_is_read(0)
                    k_products(1, 0, 2 * CH)
                    pe.wait_ge(S["v_done"], u.at("v_done", 2))
                    for t in range(QT):
                        v_tile(1, t, scb)
                    pe.wait_ge(S["v_done"], u.at("v_done", 4))
                    k_is_read(1)
                if u.kind:
                    rows = qo[:].rearrange("p n (h w) -> p n h w", w=SIDE)
                    for g in range(SIDE // 2):
                        slot = g // 2 % 2
                        if g % 2 == 0:
                            pe.wait_ge(S[f"wq_in{slot}"], u.at(f"wq_in{slot}", 16 * (3 + g // 4 + 1)))
                        if g >= 2:
                            pe.wait_ge(S["relh_done"], u.at("relh_done", g - 1))
                        for i in range(2):
                            r = 2 * g + i
                            mm = pe.matmul(scb[0:D, g % 2, i * 192:(i + 1) * 192],
                                           rel_tables(slot)[:, 0, r % RPL, :], rows[:, :, r, :],
                                           start=True, stop=True)
                        mm.then_inc(S["relh_ps"], 1)
                        if g >= 2:
                            pe.wait_ge(S["relw_done"], u.at("relw_done", g - 1))
                        for i in range(2):
                            r = 2 * g + i
                            mm = pe.matmul(maxb[D:P, g % 2, i * 192:(i + 1) * 192],
                                           rel_tables(slot)[:, 1, r % RPL, :], rows[:, :, :, r],
                                           start=True, stop=True)
                        mm.then_inc(S["relw_ps"], 1)
                        if 2 <= g < 2 + 2 * CH:
                            k_products(0, g - 2, g - 1)
                    pe.wait_ge(S["relh_done"], u.at("relh_done", 16))
                    pe.wait_ge(S["relw_done"], u.at("relw_done", 16))
                    pe.sem_inc(passed, 1)

                def max_tile(head, par, e, t, banks=(maxb,)):
                    if t == 0:
                        pe.wait_ge(S["qr_ready"], u.at("qr_ready", head * 2 + 2))
                    if u.kind == 0:
                        if t >= 2:
                            pe.wait_ge(S["max_done"], u.at("max_done", head * QT + (t - 1)))
                        lo, hi = near(t)
                        mm = pe.matmul(maxb[:, t % 2, 0:(hi - lo) * P], qr[:, t * P:(t + 1) * P],
                                       kr[:, par, e, lo * P:hi * P], start=True, stop=True)
                    else:
                        if t >= len(banks):
                            pe.wait_ge(S["max_done"], u.at("max_done", head * QT + (t + 1 - len(banks))))
                        for h in range(2):
                            mm = pe.matmul(banks[t % len(banks)][:, h, :], qr[:, t * P:(t + 1) * P],
                                           kr[:, par, e, h * HALF:(h + 1) * HALF], start=True, stop=True)
                    mm.then_inc(S["max_ps"], 1)

                def shift(head):
                    for h in range(2):
                        pe.wait_ge(S["diag_ready"], u.at("diag_ready", head * 2 + h + 1))
                        if h == 0:
                            pe.wait_ge(S["max_done"], u.at("max_done", head * QT + QT))
                        pe.matmul(maxb[:, h, :], ones_r[:], diag[:, h, :], start=True, stop=True) \
                            .then_inc(S["shift_ps"], 1)

                def values(head, par, e, n):
                    done = head * STEPS[u.kind] + n + 1
                    kt, lo, _ = steps(u.kind)[n]
                    for part, buf in (("high_done", high), ("low_done", low)):
                        pe.wait_ge(S[part], u.at(part, done))
                        if n == 0 and buf is high:
                            pe.wait_ge(S["o_act"], u.at("o_act", head))
                            pe.wait_ge(S["o_dve"], u.at("o_dve", head))
                        for a, b, first in value_parts(u.kind, n):
                            mm = pe.matmul(pvb[:, a // HALF, a % HALF:(b - 1) % HALF + 1],
                                           vop[:, par, kt, e].rearrange("p a d -> p (a d)"),
                                           buf[:, n % NR, a - lo:b - lo], start=first and buf is high, stop=True,
                                           skip_group_check=True)
                    mm.then_inc(S["value_ps"], 1)

                def row_sums(head, e):
                    pe.wait_ge(S["tallied"], u.at("tallied", (head + 1) * TALLIES[u.kind]))
                    pe.wait_ge(S["sum_act"], u.at("sum_act", head))
                    for h in range(2):
                        mm = pe.matmul(pjb[:, h, :], ones[:], tally[:, e, h * HALF:(h + 1) * HALF],
                                       start=True, stop=True)
                    mm.then_inc(S["sum_ps"], 1)

                def score(head, par, e, s):
                    if s == 0:
                        pe.wait_ge(S["shifted"], u.at("shifted", head + 1))
                        pe.wait_ge(S["qf_act"], u.at("qf_act", head + 1))
                    pe.wait_ge(S["high_done"], u.at("high_done", head * STEPS[u.kind] + (s - 1)))
                    kt, lo, hi = steps(u.kind)[s]
                    pe.matmul(scb[:, s % 2, 0:hi - lo], kop[:, par, e, kt * P:(kt + 1) * P],
                              qf[:, e, lo:hi], start=True, stop=True).then_inc(S["score_ps"], 1)

                def window(head, n, par, e, after):
                    at = PLACES[u.kind]
                    more = after or e == 0
                    for s in range(STEPS[u.kind]):
                        if s >= 2:
                            score(head, par, e, s)
                            values(head, par, e, s - 2)
                        if more:
                            for t, place in enumerate(at.maxima, 1):
                                if place == s:
                                    max_tile(head + 1, (1 - par) if e else par, 1 - e, t)
                            if s == at.shift:
                                shift(head + 1)
                        if after and e == 0 and s in at.k:
                            i = at.k.index(s)
                            if i == 0:
                                pe.wait_ge(S["sum_act"], u.at("sum_act", head))
                            k_products(n + 1, 2 * i, 2 * i + 2)
                        if after and e == 1 and s in at.v:
                            i = at.v.index(s)
                            if i == 0:
                                pe.wait_ge(S["sum_act"], u.at("sum_act", head))
                            v_tile(n + 1, i, pjb)
                    for i in range(2):
                        if more:
                            score(head + 1, (1 - par) if e else par, 1 - e, i)
                        values(head, par, e, STEPS[u.kind] - 2 + i)
                    if after:
                        max_tile(head + 2, 1 - par, e, 0)
                    if u.kind and after:
                        if e == 0:
                            k_is_read(n + 1)
                        else:
                            pe.wait_ge(S["v_done"], u.at("v_done", (n + 1) * 2 + 2))
                    row_sums(head, e)

                def pair(n, par, before, after):
                    window(n * 2, n, par, 0, after)
                    window(n * 2 + 1, n, par, 1, after)

                if u.kind:
                    for t in range(QT // 2):
                        v_tile(0, t, scb)
                    k_is_read(0)
                for t in range(QT):
                    max_tile(0, 0, 0, t, (maxb, pvb))
                    if u.kind and t % 2:
                        v_tile(0, (QT + t) // 2, scb)
                shift(0)
                score(0, 0, 0, 0)
                if u.kind:
                    pe.wait_ge(S["v_step"], u.at("v_step", 3))
                score(0, 0, 0, 1)
                max_tile(1, 0, 1, 0)
                if u.kind:
                    pe.wait_ge(S["v_done"], u.at("v_done", 2))
                pairs_of(pe, pair)

                pe.wait_ge(S["sum_act"], u.at("sum_act", HEADS))
                of_q = RAISED["wq_in0"][u.kind] // 16 - 3

                def part(c, h, first, end):
                    bank = (pjb, scb)[c % 2]
                    for i in range(first, end):
                        mm = pe.matmul(bank[:, h, :], wq[:, c % 2, i, :], qo[:, i, h * HALF:(h + 1) * HALF],
                                       start=(i == 0), stop=(i == CH - 1))
                    if end == CH:
                        mm.then_inc(S["proj_ps"], 1)

                for c in range(CH):
                    pe.wait_ge(S[f"wq_in{c % 2}"], u.at(f"wq_in{c % 2}", 16 * (of_q + c // 2 + 1)))
                    if c == 0:
                        pe.wait_ge(S["norm_done"], u.at("norm_done", PARTS * (PAIRS - 1)))
                        for h in range(2):
                            part(c, h, 0, CH - 1)
                        pe.wait_ge(S["norm_done"], u.at("norm_done", PARTS * PAIRS))
                        for h in range(2):
                            part(c, h, CH - 1, CH)
                    for h in range(2):
                        if c >= 2:
                            pe.wait_ge(S[f"added{h}"], u.at(f"added{h}", c - 1))
                        if c >= 1:
                            part(c, h, 0, CH)
                        if 2 * c + h in GN_BESIDE:
                            norm(of_next(u), GN_BESIDE.index(2 * c + h))
                for h in range(2):
                    pe.wait_ge(S[f"added{h}"], u.at(f"added{h}", CH - 1))

            units(pe, unit)

        @block.scalar
        def _(act):
            for name in LIFTED["act"]:
                act.sem_inc(S[name], START[name])
            for dst, src in ((ident[:], ident_in), (ind[:], ind_in), (indT[:], indT_in)):
                act.dma_start(dst, src).then_inc(const_in, 16)
            for parity in range(2):
                for e in range(2):
                    act.dma_start(kop[D:P, parity, e, :], onehot_in).then_inc(const_in, 16)
            act.wait_ge(S["x_in"], 16 * CH)
            for c in range(CH):
                act.dma_start(out[c * P:(c + 1) * P, :], xT_in[c * P:(c + 1) * P, :]).then_inc(copied, 16)

            def norm_root(at):
                act.wait_ge(S["gn_dve"], at("gn_dve", 9))
                act.activation(root[:], var[:], ACT.Sqrt).then_inc(S["gn_act"], 1)

            norm_root(Unit(0, 0, 0, 0).at)

            def unit(u):
                act.wait_ge(S["params_in"], u.at("params_in", RAISED["params_in"][u.kind]))
                with act.Fori(0, PAIRS) as p:
                    for h in range(2):
                        act.wait_ge(S["q_ps"], u.at("q_ps", p * 2 + h + 1))
                        act.sem_inc(passed, 1)
                        src, cols = pjb[0:D, h, :], slice(h * HALF, (h + 1) * HALF)
                        act.activation(qo[0:D, p, cols], src, ACT.Identity,
                                       bias=par[0:D, 0, bass.ds(p, 1)]).then_inc(S[f"q_act{h}"], 1)
                act.wait_ge(S["bk_ready"], u.at("bk_ready", 1))
                def k_read(n, par, h, e):
                    act.wait_ge(S["k_ps"], u.at("k_ps", n * 2 + h + 1))
                    act.sem_inc(passed, 1)
                    cols = slice(h * HALF, (h + 1) * HALF)
                    for dst in (kr, kop):
                        a = act.activation(dst[0:D, par, e, cols], pjb[e * D:(e + 1) * D, h, :], ACT.Identity,
                                           bias=bk8[e * D:(e + 1) * D, bass.ds(n, 1)], scale=0.125)
                    a.then_inc(S["k_act"], 1)

                if u.kind == 0:
                    for n in range(2):
                        for h in range(2):
                            for e in range(2):
                                k_read(n, n, h, e)
                if u.kind:
                    rows = relp[:].rearrange("r p (h w) -> r p h w", w=SIDE)
                    for g in range(SIDE // 2):
                        act.wait_ge(S["relh_ps"], u.at("relh_ps", g + 1))
                        for e in range(2):
                            src = scb[e * SIDE:(e + 1) * SIDE, g % 2, 0:2 * 192].rearrange(
                                "k (i p w) -> k i p w", i=2, w=SIDE)
                            dst = rows[e * D:e * D + SIDE, :, 2 * g:2 * g + 2, :].rearrange("k p i w -> k i p w")
                            a = act.activation(dst, src, ACT.Copy)
                        a.then_inc(S["relh_done"], 1)
                    for h in range(2):
                        for e in range(2):
                            k_read(0, 0, h, e)

                def query_operand(e, p, half):
                    act.sem_inc(passed, 1)
                    if half == 0:
                        act.activation(qf[0:D, e, :], qo[e * D:(e + 1) * D, p, :], ACT.Copy)
                    else:
                        act.activation(qf[D + SIDE:P, e, :], relp[e * D + SIDE:(e + 1) * D, p, :],
                                       ACT.Copy).then_inc(S["qf_act"], 1)

                def round_q(head, e, p):
                    act.wait_ge(S["max_ps"], u.at("max_ps", head * QT))
                    act.sem_inc(passed, 1)
                    act.activation(qr[0:D, :], qo[e * D:(e + 1) * D, p, :], ACT.Copy).then_inc(S["qr_ready"], 1)

                for h in range(2):
                    act.wait_ge(S[f"q_act{h}"], u.at(f"q_act{h}", PAIRS))
                    act.wait_ge(S[f"q_dve{h}"], u.at(f"q_dve{h}", PAIRS))
                if u.kind:
                    act.wait_ge(S["relh_done"], u.at("relh_done", 16))
                    act.wait_ge(S["relw_done"], u.at("relw_done", 16))
                else:
                    act.wait_ge(S["mask_in"], u.at("mask_in", 32))
                round_q(0, 0, 0)
                for half in range(2):
                    query_operand(0, 0, half)
                round_q(1, 1, 0)

                def exponentials(head, e, s):
                    _, lo, hi = steps(u.kind)[s]
                    done = head * STEPS[u.kind] + s
                    if u.kind and s == 0:
                        act.wait_ge(S["sum_ps"], u.at("sum_ps", head - 1))
                    if u.kind and s == 2:
                        act.wait_ge(S["sum_ps"], u.at("sum_ps", head))
                    if u.kind == 0 or s >= NP + 2:
                        act.wait_ge(S["low_done"], u.at("low_done", done - (NP - 1)))
                        act.wait_ge(S["tallied"], u.at("tallied", head * TALLIES[u.kind]
                                                       + (s - (NP - 1) - 2 * u.kind)))
                    act.wait_ge(S["score_ps"], u.at("score_ps", done + 1))
                    act.activation(raw(u.kind, e, s), scb[:, s % 2, 0:hi - lo], ACT.Exp) \
                        .then_inc(S["exp_done"], 1)
                    act.wait_ge(S["value_ps"], u.at("value_ps", done - (NR - 1)))
                    act.activation(high[:, s % NR, 0:hi - lo], scb[:, s % 2, 0:hi - lo],
                                   ACT.Exp).then_inc(S["high_done"], 1)

                def window(head, n, par, e, after):
                    at = PLACES[u.kind]
                    more = after or e == 0
                    for s in range(2, STEPS[u.kind]):
                        exponentials(head, e, s)
                        if s in at.qf and more:
                            query_operand(1 - e, n + e, at.qf.index(s))
                        if after and s == at.round_q[0]:
                            round_q(head + 2, e, n + 1)
                        if after and e == 0 and s in at.k_read:
                            k_read(n + 1, 1 - par, *divmod(at.k_read.index(s), 2))
                    if more:
                        exponentials(head + 1, 1 - e, 0)
                    act.wait_ge(S["value_ps"], u.at("value_ps", (head + 1) * STEPS[u.kind]))
                    act.sem_inc(passed, 1)
                    act.activation(qo[e * D:(e + 1) * D, n, :].rearrange("p (a b) -> p a b", a=2),
                                   pvb[0:D, :, :], ACT.Copy).then_inc(S["o_act"], 1)
                    if more:
                        exponentials(head + 1, 1 - e, 1)
                    act.wait_ge(S["sum_ps"], u.at("sum_ps", head + 1))
                    act.sem_inc(passed, 1)
                    act.activation(relp[e * D:(e + 1) * D, n, :].rearrange("p (a b) -> p a b", a=2),
                                   pjb[e * D:(e + 1) * D, :, :], ACT.Copy).then_inc(S["sum_act"], 1)

                def pair(n, par, before, after):
                    window(n * 2, n, par, 0, after)
                    window(n * 2 + 1, n, par, 1, after)

                for i in range(2):
                    exponentials(0, 0, i)
                pairs_of(act, pair)

                for c in range(CH):
                    if c == ROOT_AT:
                        norm_root(of_next(u))
                    for h in range(2):
                        act.wait_ge(S[f"added{h}"], u.at(f"added{h}", c + 1))
                    act.dma_start(out[c * P:(c + 1) * P, bass.ds(u.image * TOK, TOK)], xe[:, c % 2, :]) \
                        .then_inc(S[f"stored{c % 2}"], 16)

            units(act, unit)

        @block.vector
        def _(dve):
            for name in LIFTED["dve"]:
                dve.sem_inc(S[name], START[name])
            def norm(at, stage):
                def did(ins, step):
                    ins.then_inc(S["gn_dve"], 1)
                    dve.wait_ge(S["gn_dve"], at("gn_dve", step))
                    dve.sem_inc(passed, 1)

                if stage in (0, 1):
                    if stage == 0:
                        dve.wait_ge(S["x_in"], at("x_in", 16 * CH))
                    for c in range(stage * CH // 2, (stage + 1) * CH // 2):
                        for h in range(2):
                            a = dve.bn_stats(bst[:, c, h, :], xn[:, c, h * HALF:(h + 1) * HALF])
                    if stage == 1:
                        did(a, 1)
                        for c in range(CH):
                            a = dve.bn_aggr(mv[:, c, :], bst[:, c].rearrange("p a b -> p (a b)"))
                        did(a, 2)
                elif stage == 2:
                    dve.wait_ge(S["gn_pe"], at("gn_pe", 1))
                    did(dve.tensor_scalar(gsum[:, 0:1], maxb[0:GROUPS, 0, 0:1], 1.0 / PER_GROUP, None, ALU.mult), 3)
                elif stage == 3:
                    dve.wait_ge(S["gn_pe"], at("gn_pe", 2))
                    dve.sem_inc(passed, 1)
                    did(dve.tensor_copy(cmean[:], maxb[:, 1, 0:CH]), 4)
                    did(dve.tensor_tensor(dev[:], mv[:, :, 0], cmean[:], ALU.subtract), 5)
                    did(dve.tensor_tensor(dev[:], dev[:], dev[:], ALU.mult), 6)
                    did(dve.tensor_tensor(dev[:], dev[:], mv[:, :, 1], ALU.add), 7)
                elif stage == 4:
                    dve.wait_ge(S["gn_pe"], at("gn_pe", 3))
                    did(dve.tensor_scalar(gsum[:, 1:2], maxb[0:GROUPS, 0, 0:1], 1.0 / PER_GROUP, None, ALU.mult), 8)
                elif stage == 5:
                    dve.wait_ge(S["gn_pe"], at("gn_pe", 4))
                    did(dve.tensor_scalar(var[:], maxb[:, 1, 0:CH], GN_EPS, None, ALU.add), 9)
                else:
                    dve.wait_ge(S["gn_act"], at("gn_act", 1))
                    dve.sem_inc(passed, 1)
                    did(dve.reciprocal(rstd[:], root[:]), 10)
                    did(dve.tensor_tensor(newt[:], rstd[:], rstd[:], ALU.mult), 11)
                    did(dve.tensor_tensor(newt[:], newt[:], var[:], ALU.mult), 12)
                    did(dve.tensor_scalar(newt[:], newt[:], -0.5, 1.5, ALU.mult, ALU.add), 13)
                    did(dve.tensor_tensor(rstd[:], rstd[:], newt[:], ALU.mult), 14)
                    did(dve.scalar_tensor_tensor(nshift[:], cmean[:], -1.0, rstd[:], ALU.mult, ALU.mult), 15)
                    for c in range(CH):
                        a = dve.tensor_scalar(xn[:, c, :], xn[:, c, :], rstd[:, c:c + 1],
                                              nshift[:, c:c + 1], ALU.mult, ALU.add)
                    a.then_inc(S["xn_ready"], 1)

            for stage in range(2):
                norm(Unit(0, 0, 0, 0).at, stage)
            dve.memset(ones[:], 1.0).then_inc(const_done, 1)
            dve.wait_ge(const_in, 16 * 7)
            dve.tensor_copy(kr[D:P, :, :, :], kop[D:P, :, :, :]).then_inc(const_done, 1)
            dve.wait_ge(const_done, 2)
            dve.tensor_copy(ones_r[:], ones[:]).then_inc(const_done, 1)
            dve.wait_ge(const_done, 3)
            for stage in range(2, 7):
                norm(Unit(0, 0, 0, 0).at, stage)

            def unit(u):
                dve.wait_ge(S["params_in"], u.at("params_in", RAISED["params_in"][u.kind]))
                dve.tensor_scalar(bk8[:], par[:, 1, :], 0.125, None, ALU.mult).then_inc(S["bk_ready"], 1)
                with dve.Fori(0, PAIRS) as p:
                    for h in range(2):
                        dve.wait_ge(S["q_ps"], u.at("q_ps", p * 2 + h + 1))
                        src, cols = pjb[D:P, h, :], slice(h * HALF, (h + 1) * HALF)
                        dve.tensor_scalar(qo[D:P, p, cols], src, par[D:P, 0, bass.ds(p, 1)], None,
                                          ALU.add).then_inc(S[f"q_dve{h}"], 1)
                def v_read(n, par, g, bank):
                    dve.wait_ge(S["v_done"], u.at("v_done", n * 2 + g))
                    dve.wait_ge(S["v_ps"], u.at("v_ps", n * 2 + g + 1))
                    bias = bv[:, bass.ds(n * P, P)].rearrange("p (e d) -> p e d", e=2).unsqueeze(1)
                    dve.tensor_tensor(vraw[:], bank[:, g, :].rearrange("p (t e d) -> p t e d", t=4, e=2),
                                      bias.to_broadcast([P, 4, 2, D]), ALU.add).then_inc(S["v_step"], 1)
                    dve.wait_ge(S["v_step"], u.at("v_step", n * 4 + 2 * g + 1))
                    dve.sem_inc(passed, 1)
                    rounded, rest = (vop[:, par, 4 * g:4 * g + 4, :, part, :] for part in range(2))
                    dve.tensor_copy(rounded, vraw[:]).then_inc(S["v_step"], 1)
                    dve.wait_ge(S["v_step"], u.at("v_step", n * 4 + 2 * g + 2))
                    dve.tensor_tensor(rest, vraw[:], rounded.bitcast(F32), ALU.subtract).then_inc(S["v_done"], 1)

                if u.kind == 0:
                    for n in range(2):
                        for g in range(2):
                            v_read(n, n, g, scb)
                if u.kind:
                    rows = relp[:].rearrange("r p (h w) -> r p h w", w=SIDE)
                    for g in range(SIDE // 2):
                        dve.wait_ge(S["relw_ps"], u.at("relw_ps", g + 1))
                        for e in range(2):
                            src = maxb[D + e * SIDE:D + (e + 1) * SIDE, g % 2, 0:2 * 192].rearrange(
                                "k (i p h) -> k i p h", i=2, h=SIDE)
                            dst = rows[e * D + SIDE:(e + 1) * D, :, :, 2 * g:2 * g + 2].rearrange("k p h i -> k i p h")
                            a = dve.tensor_copy(dst, src)
                        a.then_inc(S["relw_done"], 1)

                def round_rel(head, e, p):
                    dve.wait_ge(S["max_ps"], u.at("max_ps", head * QT))
                    dve.sem_inc(passed, 1)
                    dve.tensor_copy(qr[D:P, :], relp[e * D:(e + 1) * D, p, :]).then_inc(S["qr_ready"], 1)

                def reduce(head, e, t, banks=(maxb,)):
                    dve.wait_ge(S["max_ps"], u.at("max_ps", head * QT + t + 1))
                    if u.kind == 0:
                        src = maxb[:, t % 2, 0:(near(t)[1] - near(t)[0]) * P]
                    else:
                        src = banks[t % len(banks)][:].rearrange("p a b -> p (a b)")
                    dve.tensor_reduce(negmax[:, e, t:t + 1], src, AX.X, ALU.max, negate=True) \
                        .then_inc(S["max_done"], 1)

                def shift(head, e, p):
                    dve.wait_ge(S["shift_ps"], u.at("shift_ps", head * 2 + 2))
                    rows, terms = (x.rearrange("p (a b) -> p a b", a=2)
                                   for x in (qf[D:D + SIDE, e, :], relp[e * D:e * D + SIDE, p, :]))
                    dve.tensor_tensor(rows, maxb[D:D + SIDE, :, :], terms, ALU.add).then_inc(S["shifted"], 1)

                def split(head, e, s):
                    done = head * STEPS[u.kind] + s
                    _, lo, hi = steps(u.kind)[s]
                    dve.wait_ge(S["high_done"], u.at("high_done", done + 1))
                    dve.wait_ge(S["value_ps"], u.at("value_ps", done - (NR - 1)))
                    dve.tensor_tensor(low[:, s % NR, 0:hi - lo], raw(u.kind, e, s),
                                      high[:, s % NR, 0:hi - lo].bitcast(F32), ALU.subtract) \
                        .then_inc(S["low_done"], 1)

                def add_low(head, e, p):
                    dve.wait_ge(S["o_act"], u.at("o_act", head + 1))
                    o = qo[e * D:(e + 1) * D, p, :].rearrange("p (a b) -> p a b", a=2)
                    dve.tensor_tensor(o, pvb[D:P, :, :], o, ALU.add).then_inc(S["o_dve"], 1)

                def invert(n, part):
                    if part == 0:
                        dve.wait_ge(S["o_dve"], u.at("o_dve", n * 2 + 2))
                        dve.wait_ge(S["sum_act"], u.at("sum_act", n * 2 + 2))
                        dve.sem_inc(passed, 1)
                    cols = slice(part * (TOK // PARTS), (part + 1) * (TOK // PARTS))
                    dve.reciprocal(relp[:, n, cols], relp[:, n, cols]).then_inc(S["recip_done"], 1)

                def divide(n, part):
                    dve.wait_ge(S["recip_done"], u.at("recip_done", n * PARTS + part + 1))
                    cols = slice(part * (TOK // PARTS), (part + 1) * (TOK // PARTS))
                    dve.tensor_tensor(qo[:, n, cols], qo[:, n, cols], relp[:, n, cols], ALU.mult) \
                        .then_inc(S["norm_done"], 1)

                def window(head, n, par, e, before, after):
                    at = PLACES[u.kind]
                    more = after or e == 0
                    for s in range(STEPS[u.kind]):
                        if more:
                            for t, place in enumerate(at.maxima, 1):
                                if place == s:
                                    reduce(head + 1, 1 - e, t)
                        if s >= 2:
                            split(head, e, s)
                        if more and s == at.shift:
                            shift(head + 1, 1 - e, n + e)
                        if after and s == at.round_q[1]:
                            round_rel(head + 2, e, n + 1)
                        if before and s - 1 in at.divide[e]:
                            divide(n - 1, at.divide[e].index(s - 1) + e * PARTS // 2)
                        if before and s in at.divide[e]:
                            invert(n - 1, at.divide[e].index(s) + e * PARTS // 2)
                        if after and e == 1 and s in at.v_read:
                            v_read(n + 1, 1 - par, at.v_read.index(s), pjb)
                    if more:
                        split(head + 1, 1 - e, 0)
                    if after:
                        reduce(head + 2, e, 0)
                    add_low(head, e, n)
                    if more:
                        split(head + 1, 1 - e, 1)

                def pair(n, par, before, after):
                    window(n * 2, n, par, 0, before, after)
                    window(n * 2 + 1, n, par, 1, before, after)

                for h in range(2):
                    dve.wait_ge(S[f"q_act{h}"], u.at(f"q_act{h}", PAIRS))
                    dve.wait_ge(S[f"q_dve{h}"], u.at(f"q_dve{h}", PAIRS))
                if u.kind:
                    dve.wait_ge(S["relh_done"], u.at("relh_done", 16))
                    dve.wait_ge(S["relw_done"], u.at("relw_done", 16))
                else:
                    dve.wait_ge(S["mask_in"], u.at("mask_in", 32))
                dve.sem_inc(passed, 1)
                round_rel(0, 0, 0)
                if u.kind:
                    v_read(0, 0, 0, scb)
                for t in range(QT):
                    reduce(0, 0, t, (maxb, pvb))
                round_rel(1, 1, 0)
                shift(0, 0, 0)
                if u.kind:
                    v_read(0, 0, 1, scb)
                for i in range(2):
                    split(0, 0, i)
                reduce(1, 1, 0)
                pairs_of(dve, pair)
                for part in range(PARTS):
                    invert(PAIRS - 1, part)
                    if part:
                        divide(PAIRS - 1, part - 1)
                divide(PAIRS - 1, PARTS - 1)

                for c in range(CH):
                    dve.wait_ge(S[f"xe_in{c % 2}"], u.at(f"xe_in{c % 2}", 16 * (c // 2 + 1)))
                    for h in range(2):
                        dve.wait_ge(S["proj_ps"], u.at("proj_ps", c * 2 + h + 1))
                        cols = slice(h * HALF, (h + 1) * HALF)
                        dve.scalar_tensor_tensor(xe[:, c % 2, cols], (pjb, scb)[c % 2][:, h, :], par[:, 2, c:c + 1],
                                                 xe[:, c % 2, cols], ALU.add, ALU.add).then_inc(S[f"added{h}"], 1)
                        j = 2 * c + h
                        if j in GN_AFTER:
                            norm(of_next(u), GN_AFTER.index(j))

            units(dve, unit)

        @block.gpsimd
        def _(pool):
            for name in LIFTED["pool"]:
                pool.sem_inc(S[name], START[name])
            pool.wait_ge(const_in, 16 * 7)

            def unit(u):
                def diagonals(head, e, h):
                    pool.wait_ge(S["max_done"], u.at("max_done", head * QT + 4 * h + 4))
                    pool.wait_ge(S["shift_ps"], u.at("shift_ps", head * 2))
                    pool.tensor_tensor(
                        diag[:, h, :].rearrange("p (t q) -> p t q", t=4),
                        ident[:].unsqueeze(1).to_broadcast([P, 4, P]),
                        negmax[:, e, 4 * h:4 * h + 4].unsqueeze(2).to_broadcast([P, 4, P]),
                        ALU.mult).then_inc(S["diag_ready"], 1)

                def add_up(head, e, s):
                    done = head * STEPS[u.kind] + s
                    kt, lo, hi = steps(u.kind)[s]
                    if u.kind and s < 2:
                        return
                    if u.kind == 0 and s == 0:
                        pool.wait_ge(S["sum_ps"], u.at("sum_ps", head - 1))
                    pool.wait_ge(S["exp_done"], u.at("exp_done", done + 1))
                    if u.kind and s < 4:
                        pool.wait_ge(S["low_done"], u.at("low_done", done - 1))
                    if s > 2 * u.kind:
                        pool.wait_ge(S["tallied"], u.at("tallied", head * TALLIES[u.kind] + (s - 2 * u.kind)))
                    known = hi if u.kind else max(near(kt - 1)[1] * P if kt else 0, lo)
                    src = probs[:, s % NP, :]
                    if known < hi:
                        pool.sem_inc(passed, 1)
                        a = pool.tensor_copy(tally[:, e, known:hi], src[:, known - lo:hi - lo])
                    if known > lo:
                        a = pool.tensor_tensor(tally[:, e, lo:known], tally[:, e, lo:known], src[:, 0:known - lo], ALU.add)
                    a.then_inc(S["tallied"], 1)

                def window(head, e, more):
                    for s in range(STEPS[u.kind]):
                        add_up(head, e, s)
                        if more and s in PLACES[u.kind].diag:
                            diagonals(head + 1, 1 - e, PLACES[u.kind].diag.index(s))

                def pair(n, par, before, after):
                    window(n * 2, 0, True)
                    window(n * 2 + 1, 1, after)

                for h in range(2):
                    diagonals(0, 0, h)
                pairs_of(pool, pair)

            units(pool, unit)


_SHAPES = [("xT_in", (C, IMAGES * TOK)), ("wq_in", (LAYERS, PAIRS, P, CH, P)), ("wk_in", (LAYERS, PAIRS, P, CH, P)),
           ("wv_in", (LAYERS, PAIRS, P, CH, P)), ("wo_in", (LAYERS, PAIRS, P, CH, P)),
           ("params_in", (LAYERS, P, 3, CH)), ("bv_in", (LAYERS, C)), ("rel_in", (LAYERS - 1, SIDE // RPL, P, 2, RPL, D)),
           ("onehot_in", (2 * SIDE, TOK)), ("mask_in", (2 * SIDE, TOK)), ("ident_in", (P, P)),
           ("ind_in", (P, CH, GROUPS)), ("indT_in", (GROUPS, C))]


def lay_out(inputs):
    import numpy as np

    def blocks(w):
        n = w.shape[1] // P
        full = np.zeros((PAIRS, P, CH, P), np.float32)
        full[:n] = w.reshape(CH, P, n, P).transpose(2, 1, 0, 3)
        return full

    g = {k: np.asarray(v) for k, v in inputs.items()}
    kv0 = KV_PAIRS0 * P
    wT = [g["L0_conv_w_qkv"].T, g["L1_conv_qkv_w"].T, g["L2_conv_qkv_w"].T, g["L3_conv_w_qkv"]]
    cuts = [(C, C + kv0)] + [(C, 2 * C)] * 3
    zero = np.zeros((C,), np.float32)
    qkvb = [None, g["L1_conv_qkv_b"], g["L2_conv_qkv_b"], g["L3_conv_b_qkv"]]
    ob = [zero, g["L1_conv_proj_b"], g["L2_conv_proj_b"], g["L3_conv_b_proj"]]
    wo = [g["L0_conv_w_out"].T, g["L1_conv_proj_w"].T, g["L2_conv_proj_w"].T, g["L3_conv_w_proj"]]

    def bias(i, part):
        return zero if qkvb[i] is None else qkvb[i][part * C:(part + 1) * C]

    params = np.stack([np.stack([b.reshape(CH, P).T for b in (bias(i, 0), bias(i, 1), ob[i])], axis=1)
                       for i in range(LAYERS)])
    rel = np.zeros((LAYERS - 1, P, 2, SIDE, 2, SIDE), np.float32)
    which = np.arange(SIDE)[:, None] - np.arange(SIDE)[None] + SIDE - 1
    for i, layer in ((0, "L1"), (2, "L3")):
        for a, axis in enumerate(("h", "w")):
            table = g[f"{layer}_conv_rel_pos_{axis}"][which].transpose(2, 0, 1)
            rel[i, 0:D, a, :, 0] = table
            rel[i, D:P, a, :, 1] = table
    rel = rel.reshape(LAYERS - 1, P, 2, SIDE // RPL, RPL, D).transpose(0, 3, 1, 2, 4, 5)
    row, col = np.divmod(np.arange(TOK), SIDE)
    k = np.arange(SIDE)[:, None]

    def window(at):
        first = np.clip(at - KSIZE // 2, 0, SIDE - KSIZE)[None]
        return np.where((k >= first) & (k < first + KSIZE), 0.0, MASKED)

    group = np.arange(C) // PER_GROUP
    ind = (group[:, None] == np.arange(GROUPS)).astype(np.float32)
    return {
        "xT_in": g["x"].reshape(IMAGES * TOK, C).T,
        "wq_in": np.stack([blocks(w[:, :C]) for w in wT]),
        "wk_in": np.stack([blocks(w[:, a:b]) for w, (a, b) in zip(wT, cuts)]),
        "wv_in": np.stack([blocks(w[:, b:]) for w, (a, b) in zip(wT, cuts)]),
        "wo_in": np.stack([blocks(w) for w in wo]),
        "params_in": params,
        "bv_in": np.stack([bias(i, 2) for i in range(LAYERS)]),
        "rel_in": rel,
        "onehot_in": np.concatenate([k == row, k == col]).astype(np.float32),
        "mask_in": np.concatenate([window(row), window(col)]).astype(np.float32),
        "ident_in": np.eye(P, dtype=np.float32),
        "ind_in": ind.reshape(CH, P, GROUPS).transpose(1, 0, 2),
        "indT_in": ind.T,
    }


def kernel(**inputs):
    import numpy as np
    import concourse.bacc as bacc
    from concourse.bass_utils import run_bass_kernel_spmd

    nc = bacc.Bacc("TRN2", target_bir_lowering=False, num_devices=1)
    laid = lay_out(inputs)
    arrays, args = {}, {}
    for name, shape in _SHAPES:
        arrays[name] = np.ascontiguousarray(laid[name])
        assert arrays[name].shape == shape and arrays[name].dtype == np.float32, name
        args[name] = nc.dram_tensor(name, shape, F32, kind="ExternalInput").ap()
    out = nc.dram_tensor("out", (C, IMAGES * TOK), F32, kind="ExternalOutput").ap()
    build(nc, out=out, **args)
    r = run_bass_kernel_spmd(nc, [arrays], core_ids=[0])
    return np.ascontiguousarray(r.results[0]["out"].T).reshape(IMAGES, SIDE, SIDE, C)
```
